# Optimizing a Trainium2 kernel written in Bass

```python
import numpy as np
import jax
import jax.numpy as jnp

def _softmax(x, axis=-1):
    return jax.nn.softmax(x, axis=axis)

def _gelu(x):
    return jax.nn.gelu(x, approximate=True)

def _silu(x):
    return jax.nn.silu(x)

def _sigmoid(x):
    return jax.nn.sigmoid(x)

def _layernorm(x, axis=-1, eps=1e-05):
    m = jnp.mean(x, axis=axis, keepdims=True)
    v = jnp.var(x, axis=axis, keepdims=True)
    return (x - m) / jnp.sqrt(v + eps)

def _scatter_add(tgt, idx, src, axis=0):
    return tgt.at[idx].add(src)

def _segment_sum(src, seg, n):
    return jax.ops.segment_sum(src, seg, n)
kernel_name = 'mk_conv_preact_d4_conv_nchw64_r2_d1e8b8'

def setup_inputs(seed: int=0):
    np.random.seed(seed)
    _w = jnp.asarray

    def _rec_inputs():
        import jax
        import jax.numpy as jnp
        _gk = jax.random.key(seed)
        x = 7.22e-05 + 1 * jax.random.normal(jax.random.fold_in(_gk, 1), (32, 32, 32, 32), jnp.float32)
        return x
    x = _rec_inputs()

    def _L0_conv_setup():
        import jax, jax.numpy as jnp
        import numpy as np
        PS = 8
        E = 8

        def patchify(x, ps):
            B, C, h, w = x.shape
            nv, nh = (h // ps, w // ps)
            xp = jnp.pad(x, ((0, 0), (0, 0), (1, 1), (1, 1)))
            k = ps + 2
            iv = jnp.arange(nv)[:, None] * ps + jnp.arange(k)[None, :]
            ih = jnp.arange(nh)[:, None] * ps + jnp.arange(k)[None, :]
            win = xp[:, :, iv[:, None, :, None], ih[None, :, None, :]]
            return win.reshape(B * nv * nh, C, k, k)

        def unpatchify(y, h, w, ps):
            y = y[:, :, 1:-1, 1:-1]
            nv, nh = (h // ps, w // ps)
            C = y.shape[1]
            p = y.reshape(-1, C, nv * nh, ps * ps)
            B = p.shape[0]
            p = p.transpose(0, 1, 3, 2)
            p = p.reshape(B, C, ps, ps, nv, nh)
            p = p.transpose(0, 1, 4, 2, 5, 3)
            return p.reshape(B, C, h, w)
        key = jax.random.key(seed)
        k1, k2, k3 = jax.random.split(key, 3)
        C = 32
        x = jax.random.normal(k1, (32, C, 32, 32), dtype=jnp.float32)
        Wg = jax.random.normal(k2, (C, E), dtype=jnp.float32) * 0.05
        bg = jnp.zeros((E,), dtype=jnp.float32)
        Wexp = jax.random.normal(k3, (E, C, C, 3, 3), dtype=jnp.float32) * 0.05
        bexp = jnp.zeros((E, C), dtype=jnp.float32)
        return {'x': x, 'Wg': Wg, 'bg': bg, 'Wexp': Wexp, 'bexp': bexp}
    _L0_conv_all = _L0_conv_setup()
    _L0_conv_in = {k: v for k, v in _L0_conv_all.items() if k in ('Wg', 'bg', 'Wexp', 'bexp')}
    del _L0_conv_all

    def _L1_conv_setup():
        import jax, jax.numpy as jnp
        import numpy as np
        B, C_IN, H, W = (32, 32, 64, 64)
        C_OUT, E, K = (32, 4, 3)
        key = jax.random.key(seed)
        k1, k2, k3, k4 = jax.random.split(key, 4)
        x = jax.random.normal(k1, (B, C_IN, H, W), dtype=jnp.float32)
        w_route = jax.random.normal(k2, (E, C_IN), dtype=jnp.float32) * (1.0 / np.sqrt(C_IN))
        b_route = jax.random.normal(k3, (E,), dtype=jnp.float32) * 0.01
        fan_in = C_IN * K * K
        w_experts = jax.random.normal(k4, (E, C_OUT, C_IN, K, K), dtype=jnp.float32) * (1.0 / np.sqrt(fan_in))
        return {'x': x, 'w_route': w_route, 'b_route': b_route, 'w_experts': w_experts}
    _L1_conv_all = _L1_conv_setup()
    _L1_conv_in = {k: v for k, v in _L1_conv_all.items() if k in ('w_route', 'b_route', 'w_experts')}
    del _L1_conv_all

    def _L2_conv_setup():
        import jax, jax.numpy as jnp
        import numpy as np
        NUM_EMBEDDINGS = 512
        EMBEDDING_DIM = 32
        COMMITMENT_COST = 0.25
        key = jax.random.key(seed)
        k1, k2 = jax.random.split(key)
        B, D, H, W = (32, EMBEDDING_DIM, 32, 32)
        inputs = jax.random.normal(k1, (B, D, H, W), dtype=jnp.float32)
        lim = 1.0 / NUM_EMBEDDINGS
        codebook = jax.random.uniform(k2, (NUM_EMBEDDINGS, EMBEDDING_DIM), dtype=jnp.float32, minval=-lim, maxval=lim)
        return {'inputs': inputs, 'codebook': codebook}
    _L2_conv_all = _L2_conv_setup()
    _L2_conv_in = {k: v for k, v in _L2_conv_all.items() if k in ('codebook',)}
    del _L2_conv_all

    def _L3_conv_setup():
        import jax, jax.numpy as jnp
        import numpy as np
        K = 3

        def _bilinear_sample_one(img, px, py):
            C, H, W = img.shape
            x0 = jnp.floor(px)
            y0 = jnp.floor(py)
            x1 = x0 + 1.0
            y1 = y0 + 1.0
            wx1 = px - x0
            wx0 = 1.0 - wx1
            wy1 = py - y0
            wy0 = 1.0 - wy1

            def tap(xi, yi, w):
                valid = (xi >= 0) & (xi <= W - 1) & (yi >= 0) & (yi <= H - 1)
                xc = jnp.clip(xi, 0, W - 1).astype(jnp.int32)
                yc = jnp.clip(yi, 0, H - 1).astype(jnp.int32)
                v = img[:, yc, xc]
                return v * (w * valid)[None]
            return tap(x0, y0, wx0 * wy0) + tap(x1, y0, wx1 * wy0) + tap(x0, y1, wx0 * wy1) + tap(x1, y1, wx1 * wy1)
        key = jax.random.key(seed)
        k1, k2, k3 = jax.random.split(key, 3)
        N, C_in, C_out, H, W = (8, 32, 32, 64, 64)
        inputs = jax.random.normal(k1, (N, C_in, H, W), dtype=jnp.float32)
        w_grid = jax.random.normal(k2, (2 * K * K, C_in), dtype=jnp.float32) * 0.01
        b_grid = jnp.zeros((2 * K * K,), dtype=jnp.float32)
        w_conv = jax.random.normal(k3, (C_out, C_in, K, K), dtype=jnp.float32) / np.sqrt(C_in * K * K)
        return {'inputs': inputs, 'w_grid': w_grid, 'b_grid': b_grid, 'w_conv': w_conv}
    _L3_conv_all = _L3_conv_setup()
    _L3_conv_in = {k: v for k, v in _L3_conv_all.items() if k in ('w_grid', 'b_grid', 'w_conv')}
    del _L3_conv_all
    return {'x': x, 'L0_conv_Wg': _L0_conv_in['Wg'], 'L0_conv_bg': _L0_conv_in['bg'], 'L0_conv_Wexp': _L0_conv_in['Wexp'], 'L0_conv_bexp': _L0_conv_in['bexp'], 'L1_conv_w_route': _L1_conv_in['w_route'], 'L1_conv_b_route': _L1_conv_in['b_route'], 'L1_conv_w_experts': _L1_conv_in['w_experts'], 'L2_conv_codebook': _L2_conv_in['codebook'], 'L3_conv_w_grid': _L3_conv_in['w_grid'], 'L3_conv_b_grid': _L3_conv_in['b_grid'], 'L3_conv_w_conv': _L3_conv_in['w_conv']}

def reference(x, L0_conv_Wg, L0_conv_bg, L0_conv_Wexp, L0_conv_bexp, L1_conv_w_route, L1_conv_b_route, L1_conv_w_experts, L2_conv_codebook, L3_conv_w_grid, L3_conv_b_grid, L3_conv_w_conv):
    import jax
    import jax.numpy as jnp

    def _L0_conv_ref(x, Wg, bg, Wexp, bexp):
        import jax, jax.numpy as jnp
        import numpy as np
        PS = 8
        E = 8

        def patchify(x, ps):
            B, C, h, w = x.shape
            nv, nh = (h // ps, w // ps)
            xp = jnp.pad(x, ((0, 0), (0, 0), (1, 1), (1, 1)))
            k = ps + 2
            iv = jnp.arange(nv)[:, None] * ps + jnp.arange(k)[None, :]
            ih = jnp.arange(nh)[:, None] * ps + jnp.arange(k)[None, :]
            win = xp[:, :, iv[:, None, :, None], ih[None, :, None, :]]
            return win.reshape(B * nv * nh, C, k, k)

        def unpatchify(y, h, w, ps):
            y = y[:, :, 1:-1, 1:-1]
            nv, nh = (h // ps, w // ps)
            C = y.shape[1]
            p = y.reshape(-1, C, nv * nh, ps * ps)
            B = p.shape[0]
            p = p.transpose(0, 1, 3, 2)
            p = p.reshape(B, C, ps, ps, nv, nh)
            p = p.transpose(0, 1, 4, 2, 5, 3)
            return p.reshape(B, C, h, w)
        B, C, H, W = x.shape
        v_pad = PS - H % PS
        h_pad = PS - W % PS
        x = jnp.pad(x, ((0, 0), (0, 0), (0, v_pad), (0, h_pad)))
        h, w = (x.shape[2], x.shape[3])
        patched = patchify(x, PS)
        feat = patched.mean(axis=(2, 3))
        logits = feat @ Wg + bg
        probs = jax.nn.softmax(logits, axis=-1)
        routing = jax.nn.one_hot(jnp.argmax(logits, axis=-1), E, dtype=probs.dtype) * probs

        def expert(w_, b_):
            y = jax.lax.conv_general_dilated(patched, w_, (1, 1), 'SAME', dimension_numbers=('NCHW', 'OIHW', 'NCHW'))
            return jax.nn.relu(y + b_[None, :, None, None])
        outs = jax.vmap(expert)(Wexp, bexp)
        combined = jnp.einsum('ne,encij->ncij', routing, outs)
        y = unpatchify(combined, h, w, PS)
        return y[:, :, :H, :W]

    def _L1_conv_ref(x, w_route, b_route, w_experts):
        import jax, jax.numpy as jnp
        import numpy as np
        B, C_IN, H, W = (32, 32, 64, 64)
        C_OUT, E, K = (32, 4, 3)
        pooled = jnp.mean(x, axis=(2, 3))
        routing = jax.nn.sigmoid(pooled @ w_route.T + b_route)
        w_mixed = jnp.einsum('be,eoihw->boihw', routing, w_experts)

        def conv_one(xi, wi):
            return jax.lax.conv_general_dilated(xi[None], wi, window_strides=(1, 1), padding='SAME', dimension_numbers=('NCHW', 'OIHW', 'NCHW'))[0]
        y = jax.vmap(conv_one)(x, w_mixed)
        return y

    def _L2_conv_ref(inputs, codebook):
        import jax, jax.numpy as jnp
        import numpy as np
        NUM_EMBEDDINGS = 512
        EMBEDDING_DIM = 32
        COMMITMENT_COST = 0.25
        x = jnp.transpose(inputs, (0, 2, 3, 1))
        input_shape = x.shape
        flat = x.reshape(-1, EMBEDDING_DIM)
        distances = jnp.sum(flat * flat, axis=1, keepdims=True) + jnp.sum(codebook * codebook, axis=1) - 2.0 * flat @ codebook.T
        indices = jnp.argmin(distances, axis=1)
        quantized = codebook[indices].reshape(input_shape)
        quantized = x + jax.lax.stop_gradient(quantized - x)
        return jnp.transpose(quantized, (0, 3, 1, 2))

    def _L3_conv_ref(inputs, w_grid, b_grid, w_conv):
        import jax, jax.numpy as jnp
        import numpy as np
        K = 3

        def _bilinear_sample_one(img, px, py):
            C, H, W = img.shape
            x0 = jnp.floor(px)
            y0 = jnp.floor(py)
            x1 = x0 + 1.0
            y1 = y0 + 1.0
            wx1 = px - x0
            wx0 = 1.0 - wx1
            wy1 = py - y0
            wy0 = 1.0 - wy1

            def tap(xi, yi, w):
                valid = (xi >= 0) & (xi <= W - 1) & (yi >= 0) & (yi <= H - 1)
                xc = jnp.clip(xi, 0, W - 1).astype(jnp.int32)
                yc = jnp.clip(yi, 0, H - 1).astype(jnp.int32)
                v = img[:, yc, xc]
                return v * (w * valid)[None]
            return tap(x0, y0, wx0 * wy0) + tap(x1, y0, wx1 * wy0) + tap(x0, y1, wx0 * wy1) + tap(x1, y1, wx1 * wy1)
        N, C, H, W = inputs.shape
        k = K
        off = jnp.einsum('nchw,oc->nohw', inputs, w_grid) + b_grid[None, :, None, None]
        off = off.transpose(0, 2, 3, 1).reshape(N, H, W, k, k, 2)
        base_x = jnp.linspace(-1.0, 1.0, W)
        base_y = jnp.linspace(-1.0, 1.0, H)
        koff_x = jnp.linspace(-(k - 1) / (W - 1), (k - 1) / (W - 1), k)
        koff_y = jnp.linspace(-(k - 1) / (H - 1), (k - 1) / (H - 1), k)
        gx = base_x[None, None, :, None, None] + koff_x[None, None, None, None, :] + off[..., 0]
        gy = base_y[None, :, None, None, None] + koff_y[None, None, None, :, None] + off[..., 1]
        gx = gx.transpose(0, 1, 3, 2, 4).reshape(N, H * k, W * k)
        gy = gy.transpose(0, 1, 3, 2, 4).reshape(N, H * k, W * k)
        px = (gx + 1.0) * 0.5 * (W - 1)
        py = (gy + 1.0) * 0.5 * (H - 1)
        sampled = jax.vmap(_bilinear_sample_one)(inputs, px, py)
        out = jax.lax.conv_general_dilated(sampled, w_conv, window_strides=(k, k), padding='VALID', dimension_numbers=('NCHW', 'OIHW', 'NCHW'))
        return out

    def _gn(v, G=32, eps=1e-05):
        B_, C_, H_, W_ = v.shape
        g = v.reshape(B_, G, C_ // G, H_, W_)
        m = jnp.mean(g, axis=(2, 3, 4), keepdims=True)
        s = jnp.var(g, axis=(2, 3, 4), keepdims=True)
        return ((g - m) / jnp.sqrt(s + eps)).reshape(v.shape)

    def _ln_c(v, eps=1e-06):
        m = jnp.mean(v, axis=1, keepdims=True)
        s = jnp.var(v, axis=1, keepdims=True)
        return (v - m) / jnp.sqrt(s + eps)

    def _ln_t(v, eps=1e-05):
        m = jnp.mean(v, axis=-1, keepdims=True)
        s = jnp.var(v, axis=-1, keepdims=True)
        return (v - m) / jnp.sqrt(s + eps)

    def _to_tokens(v):
        B_, C_, H_, W_ = v.shape
        return v.reshape(B_, C_, H_ * W_).transpose(0, 2, 1)

    def _from_tokens(t, like):
        B_, C_, H_, W_ = like.shape
        return t.transpose(0, 2, 1).reshape(B_, C_, H_, W_)
    x = x + _L0_conv_ref(_gn(x), L0_conv_Wg, L0_conv_bg, L0_conv_Wexp, L0_conv_bexp)
    x = x + _L1_conv_ref(_gn(x), L1_conv_w_route, L1_conv_b_route, L1_conv_w_experts)
    x = x + _L2_conv_ref(_gn(x), L2_conv_codebook)
    x = x + _L3_conv_ref(_gn(x), L3_conv_w_grid, L3_conv_b_grid, L3_conv_w_conv)
    return x

_drawn_inputs = setup_inputs


def setup_inputs(seed=0):
    import zlib

    import numpy as np

    out = dict(_drawn_inputs(seed))
    spreads = {'L0_conv_bg': (0.0, 0.1), 'L0_conv_bexp': (0.0, 0.644), 'L3_conv_b_grid': (0.0, 0.1)}
    factors = {'L1_conv_w_route': 64.0, 'L1_conv_b_route': 8.0, 'L2_conv_codebook': 57.51}
    for name, (base, spread) in spreads.items():
        noise = np.random.default_rng([zlib.crc32(name.encode()), seed]).standard_normal(out[name].shape)
        drawn = base * np.exp(spread * noise) if base else spread * noise
        out[name] = jnp.asarray(drawn.astype(out[name].dtype))
    for name, factor in factors.items():
        out[name] = (out[name] * factor).astype(out[name].dtype)
    return out
```

```python
from contextlib import ExitStack

import numpy as np

import concourse.bass as bass
from concourse import mybir

ALU = mybir.AluOpType
ACT = mybir.ActivationFunctionType
AX = mybir.AxisListType
F32 = mybir.dt.float32
I32 = mybir.dt.int32
U32 = mybir.dt.uint32

B, C, H, W = 32, 32, 32, 32
PIX = H * W
IMG = 4
GROUPS = B // IMG
P = IMG * C
PS = 8
NV = H // PS + 1
PATCHES = NV * NV
WIN = PS + 2
G0 = NV * PS + 2
WROW = WIN * WIN + 1
CUT = PS * WIN + 1
E0 = 8
HALF = 4
ROWN = NV * PS * PS
E1 = 4
G1 = W + 2
TAPS = 9
CODES = 512
CCH = CODES // 128
TILES = PIX // 128
CORN = 4
TROWS = 9 * 128
XP3 = TROWS + G1 + 2
ROW = TAPS * CORN * C
TC = TAPS * C
EPS = 1e-5
AHEAD = 3
STORED_AHEAD = 16 * (IMG + 1)

INPUTS = ["x", "Wg", "bg", "Wexp", "bexp", "w_route", "b_route", "w_mix", "codebook", "codebook_t",
          "w_grid", "b_grid", "w_conv", "ident", "pick_expert", "sum_experts", "same_image",
          "code_iota", "first_rank", "grid"]


def build(nc, A, out):
    ctx = ExitStack()
    with ctx:
        def sb(name, shape, dt=F32):
            return ctx.enter_context(nc.sbuf_tensor(name, shape, dt))

        def bank(name):
            return ctx.enter_context(nc.psum_tensor(name, [128, 512], F32))

        def sem(name):
            return ctx.enter_context(nc.semaphore(name))

        ident = sb("ident_sb", [128, 128])
        pick = sb("pick_sb", [IMG * E0, 2 * IMG, 128])
        sume = sb("sume_sb", [128, C])
        same = sb("same_sb", [128, 128])
        iota = sb("iota_sb", [128, CODES])
        rank = sb("rank_sb", [PATCHES, IMG, E0])
        grid = sb("grid_sb", [128, 2, TILES * TAPS])
        w0 = sb("w0", [3 * C, 3, 2, 128])
        bexp = sb("bexp_sb", [128, 2])
        wg = sb("wg_sb", [3 * C, E0])
        bg = sb("bg_sb", [PATCHES, IMG, E0])
        wmix = sb("wmix", [128, E1, TC])
        wroute = sb("wroute", [128, E1])
        broute = sb("broute", [128, E1])
        cb2 = sb("cb2", [C + 1, CODES])
        cbsq = sb("cbsq", [C, CODES])
        negone = sb("negone", [C, 1])
        codes = sb("codes", [128, CCH, C])
        wgrid = sb("wgrid", [128, IMG * 2 * TAPS])
        bgrid = sb("bgrid", [128, 2 * TAPS])
        wc = sb("wc", [128, 3, C])
        xres = sb("xres", [128, PIX])
        xfin = sb("xfin", [128, PIX])
        xlast = sb("xlast", [128, PIX])
        stats = sb("stats", [128, 2, 6])
        mv = sb("mv", [128, 2])
        ve = sb("ve", [128, 1])
        sd = sb("sd", [128, 1])
        nr = sb("nr", [128, 4])
        xp0 = sb("xp0", [128, G0 * G0])
        arena = sb("arena", [128, IMG * PATCHES * CUT])
        xs0 = arena[0:3 * C, :].rearrange("p (i n s) -> p i n s", i=IMG, s=CUT)
        onehot = arena[:, 0:2 * CODES].rearrange("p (b n) -> p b n", b=2)
        onehot_t = arena[:, 2 * CODES:4 * CODES].rearrange("p (b n) -> p b n", b=2)
        o3 = 4 * CODES
        xs3 = arena[:, o3:o3 + 2 * TROWS].rearrange("p (b n) -> p b n", b=2)
        o3 += 2 * TROWS
        cells = arena[:, o3:o3 + TROWS]
        rowsum = sb("rowsum", [128, G0, NV])
        lg = sb("lg", [PATCHES, 6, IMG, E0])
        mx = sb("mx", [PATCHES, 3, IMG])
        rt_t = sb("rt_t", [IMG * E0, PATCHES])
        rtb = sb("rtb", [128, 2 * IMG, PATCHES])
        ex0 = sb("ex0", [128, 2, 2, ROWN])
        blocks = sb("blocks", [128, 2 * NV * ROWN])
        win = blocks[:, 0:PATCHES * WROW].rearrange("p (n s) -> p n s", s=WROW)
        yc = blocks[:, 0:NV * ROWN]
        yb = blocks[:, NV * ROWN:2 * NV * ROWN]
        xp1 = sb("xp1", [128, G1 * G1])
        sm1 = sb("sm1", [128, 4, E1])
        mix = sb("mix", [128, TC])
        bd1 = sb("bd1", [128, TAPS, 128])
        xn2 = sb("xn2", [128, PIX])
        xs2 = sb("xs2", [C + 1, 2, 128])
        top = sb("top", [128, 2, 8])
        code = sb("code", [128, 2, 8], U32)
        q2 = sb("q2", [128, PIX])
        xp3 = sb("xp3", [128, XP3])
        NK = IMG * TILES * TAPS
        pos = sb("pos", [128, 2, IMG, TILES * TAPS])
        cell_i = sb("cell_i", [128, 2 * NK], I32)
        cell = sb("cell", [128, 2, NK])
        over = sb("over", [128, 2, NK])
        idx = sb("idx_sb", [128, IMG, TILES, TAPS])
        wq = sb("wq", [128, IMG, TILES, TAPS * CORN])
        idx_slot = sb("idx_slot", [128, TILES, TAPS], U32)
        w_slot = sb("w_slot", [128, TILES, TAPS * CORN])
        ring = sb("ring", [128, TILES, ROW])
        pair = sb("pair", [128, TAPS, 2, C])
        samp = sb("samp", [128, 2, TC])
        samp_t = sb("samp_t", [128, 3, 256])
        fin = sb("fin", [128, PIX])

        P0, P1, P2, P3, P4, PT, PT2, PO = [bank(f"bank{n}") for n in range(8)]
        PP = [P0, P1, P2, P3]

        win_dram = nc.dram_tensor("windows", [IMG, C * PATCHES, WROW], F32).ap()
        y_dram = nc.dram_tensor("y_patches", [IMG, C * PATCHES, PS * PS], F32).ap()
        table = [nc.dram_tensor(f"cells_{i}", [TROWS, CORN * C], F32).ap() for i in range(IMG)]

        loaded = sem("loaded")
        zeroed = sem("zeroed")
        sq_ready = sem("sq_ready")
        norms_ready = sem("norms_ready")
        x_loaded = sem("x_loaded")
        x3_ready = sem("x3_ready")
        var_ready = sem("var_ready")
        sd_ready = sem("sd_ready")
        win_ready = sem("win_ready")
        win_out = sem("win_out")
        xs0_loaded = sem("xs0_loaded")
        logit_ready = sem("logit_ready")
        diff_ready = sem("diff_ready")
        exp_ready = sem("exp_ready")
        route_ready = sem("route_ready")
        route_t = sem("route_t")
        route_t_sb = sem("route_t_sb")
        route_b = sem("route_b")
        conv0_done = sem("conv0_done")
        relu_done = sem("relu_done")
        gated = sem("gated")
        sum0_done = sem("sum0_done")
        yc_done = sem("yc_done")
        y_out = sem("y_out")
        y_in = sem("y_in")
        pooled = sem("pooled")
        rlog_ready = sem("rlog_ready")
        z_ready = sem("z_ready")
        ez_ready = sem("ez_ready")
        bd_ready = sem("bd_ready")
        conv1_done = sem("conv1_done")
        x2_ready = sem("x2_ready")
        xn2_ready = sem("xn2_ready")
        staged2 = sem("staged2")
        score_done = sem("score_done")
        onehot_ready = sem("onehot_ready")
        turned = sem("turned")
        turned_sb = sem("turned_sb")
        q_done = sem("q_done")
        q_sb = sem("q_sb")
        xn3_ready = sem("xn3_ready")
        flat3_ready = sem("flat3_ready")
        off_done = sem("off_done")
        off_read = sem("off_read")
        xs3_loaded = sem("xs3_loaded")
        cells_t = sem("cells_t")
        cells_sb = sem("cells_sb")
        tabled = [sem(f"tabled{i}") for i in range(IMG)]
        granted = sem("granted")
        gathered = [sem(f"gathered{t}") for t in range(TILES)]
        samp_ready = sem("samp_ready")
        samp_turned = sem("samp_turned")
        samp_sb = sem("samp_sb")
        conv3_done = sem("conv3_done")
        fin_ready = sem("fin_ready")
        stored = sem("stored")

        pe_passed, dve_passed = sem("pe_passed"), sem("dve_passed")
        pool_passed, sp_passed = sem("pool_passed"), sem("sp_passed")

        block = ctx.enter_context(nc.Block())

        def schedule(eng, front, late, back):
            for part in front:
                part(0)
            late(0)
            with eng.Fori(0, GROUPS - 1) as g:
                for i in range(IMG):
                    back(g, i, stage=True)
                    if i < IMG - 1:
                        front[i](g + 1)
                late(g + 1)
            for i in range(IMG):
                back(GROUPS - 1, i, stage=i < IMG - 1)

        def view0(t, i, v):
            pass

        @block.sync
        def _(sp):
            sp.sem_inc(stored, STORED_AHEAD)
            for dst, src in (
                (ident[:], A["ident"]), (pick[:], A["pick_expert"]), (sume[:], A["sum_experts"]),
                (same[:], A["same_image"]), (rank[:], A["first_rank"]), (grid[:], A["grid"]),
                (w0[:], A["Wexp"]), (bexp[:], A["bexp"]), (bg[:], A["bg"].partition_broadcast(PATCHES)),
            ):
                sp.dma_start(dst, src).then_inc(loaded, 16)
            sp.wait_ge(zeroed, 1)
            for i in range(IMG):
                r = slice(C * i, C * (i + 1))
                sp.dma_start(wgrid[r, 2 * TAPS * i:2 * TAPS * (i + 1)], A["w_grid"]).then_inc(loaded, 16)
            sp.dma_start(wg[2 * C:3 * C, :], A["Wg"]).then_inc(loaded, 16)

            def load_x(g):
                sp.wait_ge(x3_ready, g)
                sp.dma_start(xres[:], A["x"].rearrange("(g p) n -> g p n", p=P)[bass.ds(g, 1)]
                             .rearrange("g p n -> (g p) n")).then_inc(x_loaded, 16)

            def front0(g):
                if isinstance(g, int):
                    load_x(g)
                sp.wait_ge(win_ready, g + 1)
                sp.sem_inc(sp_passed, 1)
                sp.wait_ge(xs0_loaded, 16 * 3 * IMG * g)
                sp.sem_inc(sp_passed, 1)
                sp.dma_start(win_dram.rearrange("i (c n) s -> (i c) (n s)", c=C),
                             win.rearrange("p n s -> p (n s)")).then_inc(win_out, 16)
                sp.wait_ge(win_out, 16 * (g + 1))
                sp.sem_inc(sp_passed, 1)
                sp.wait_ge(tabled[IMG - 1], 16 * g)
                sp.sem_inc(sp_passed, 1)
                for i in range(IMG):
                    for dy in range(3):
                        n = CUT if dy == 2 else CUT - 1
                        sp.dma_start(xs0[C * dy:C * (dy + 1), i, :, 0:n],
                                     win_dram[i].rearrange("(p c) s -> c p s", c=C)[:, :, dy * WIN:dy * WIN + n]
                                     ).then_inc(xs0_loaded, 16)
                sp.wait_ge(yc_done, NV * (g + 1) + AHEAD)
                sp.wait_ge(y_in, 16 * g)
                for i in range(IMG):
                    sp.dma_start(y_dram[i].rearrange("(p c) s -> c p s", c=C),
                                 yc[C * i:C * (i + 1), :].rearrange("c (p s) -> c p s", s=PS * PS)
                                 ).then_inc(y_out, 16)
                sp.wait_ge(y_out, 16 * IMG * (g + 1))
                sp.dma_start(yb[:], y_dram.rearrange("i (c n) s -> (i c) (n s)", c=C)).then_inc(y_in, 16)

            def front1(g):
                pass

            def write_table(g, i):
                sp.wait_ge(xn3_ready, g + 1)
                if i >= 2:
                    sp.wait_ge(cells_t, IMG * g + i - 1)
                for q in range(CORN):
                    f = (q // 2) * G1 + q % 2
                    sp.dma_start(xs3[C * q:C * (q + 1), i % 2, :],
                                 xp3[C * i:C * (i + 1), f:f + TROWS]).then_inc(xs3_loaded, 16)
                sp.wait_ge(cells_sb, 3 * (IMG * g + i + 1))
                sp.sem_inc(sp_passed, 1)
                if isinstance(g, int):
                    assert g == 0
                else:
                    sp.wait_ge(samp_ready, TILES * (IMG * (g - 1) + i + 1))
                    sp.sem_inc(sp_passed, 1)
                sp.dma_start(table[i].rearrange("(n p) c -> p n c", p=128),
                             cells.rearrange("p (n c) -> p n c", c=128)).then_inc(tabled[i], 16)

            def front2(g):
                for i in range(IMG - 1):
                    write_table(g, i)

            def late(g):
                write_table(g, IMG - 1)

            def back(g, i, stage):
                if i == 0 and not isinstance(g, int):
                    load_x(g + 1)
                sp.wait_ge(fin_ready, TILES // 2 * (IMG * g + i + 1) + AHEAD)
                sp.wait_ge(stored, 16 * (IMG * g + i) + STORED_AHEAD)
                rows = A["out"].rearrange("(n p) m -> n p m", p=C)
                sp.dma_start(rows[bass.ds(IMG * g + i, 1)].rearrange("n p m -> (n p) m"),
                             fin[C * i:C * (i + 1), :]).then_inc(stored, 16)

            schedule(sp, [front0, front1, front2], late, back)
            sp.wait_ge(stored, 16 * B + STORED_AHEAD)

        @block.gpsimd
        def _(pool):
            with pool.Fori(0, GROUPS) as g:
                for i in range(IMG):
                    pool.wait_ge(tabled[i], 16 * (g + 1))
                    for t in range(TILES):
                        pool.wait_ge(granted, IMG * TILES * g + TILES * i + t + 1)
                        pool.sem_inc(pool_passed, 1)
                        for k in range(TAPS):
                            pool.indirect_dma_start(
                                ring[:, t, CORN * C * k:CORN * C * (k + 1)], None, table[i],
                                bass.IndirectOffsetOnAxis(ap=idx_slot[:, t, k:k + 1], axis=0),
                            ).then_inc(gathered[t], 16)

        @block.scalar
        def _(act):
            for i in range(IMG):
                r = slice(C * i, C * (i + 1))
                act.dma_start(wmix[r], A["w_mix"]).then_inc(loaded, 16)
                act.dma_start(wroute[r], A["w_route"]).then_inc(loaded, 16)
            act.dma_start(broute[:], A["b_route"].partition_broadcast(128)).then_inc(loaded, 16)
            act.dma_start(cb2[0:C, :], A["codebook_t"]).then_inc(loaded, 16)
            act.dma_start(codes[:], A["codebook"].rearrange("(k p) c -> p k c", p=128)).then_inc(loaded, 16)
            act.dma_start(iota[:], A["code_iota"]).then_inc(loaded, 16)
            act.dma_start(bgrid[:], A["b_grid"].partition_broadcast(128)).then_inc(loaded, 16)
            for r in range(3):
                n = min(128, TC - 128 * r)
                act.dma_start(wc[0:n, r, :], A["w_conv"][128 * r:128 * r + n, :]).then_inc(loaded, 16)
            act.wait_ge(loaded, LOADS)
            act.sem_inc(relu_done, AHEAD)
            act.sem_inc(turned_sb, AHEAD)
            act.sem_inc(yc_done, AHEAD)
            act.sem_inc(q_sb, AHEAD)
            act.sem_inc(samp_sb, AHEAD)

            def root(g, n):
                act.wait_ge(var_ready, 4 * g + n + 1)
                act.activation(sd[:], ve[:], ACT.Sqrt).then_inc(sd_ready, 1)

            def front0(g):
                root(g, 0)
                act.wait_ge(diff_ready, g + 1)
                act.activation(lg[:, 2], lg[:, 1], ACT.Exp).then_inc(exp_ready, 1)

                def row(v):
                    for i in range(IMG):
                        n = IMG * (NV * g + v) + i
                        for h in range(2):
                            act.wait_ge(conv0_done, 2 * n + h + 1)
                            if h == 0:
                                act.wait_ge(sum0_done, n - 1 + AHEAD)
                            act.activation(ex0[:, i % 2, h, :], PP[2 * (i % 2) + h][:, 0:ROWN], ACT.Relu,
                                           bias=bexp[:, h:h + 1]).then_inc(relu_done, 1)
                    act.wait_ge(sum0_done, IMG * (NV * g + v + 1) + AHEAD)
                    act.wait_ge(win_out, 16 * (g + 1))
                    act.copy(yc[:, bass.ds(v * ROWN, ROWN)], P4[:, 0:ROWN]).then_inc(yc_done, 1)
                with act.Fori(0, NV) as v:
                    row(v)

            def front1(g):
                root(g, 1)
                act.wait_ge(z_ready, g + 1)
                act.activation(sm1[:, 2, :], sm1[:, 1, :], ACT.Exp, scale=-1.0).then_inc(ez_ready, 1)
                root(g, 2)
                act.wait_ge(xn2_ready, g + 1)

                def stage(t, i):
                    n = IMG * (TILES * g + t) + i
                    act.wait_ge(score_done, n - 1 + AHEAD)
                    act.copy(xs2[0:C, i % 2, :], xn2[C * i:C * (i + 1), bass.ds(128 * t, 128)]
                             ).then_inc(staged2, 1)

                def turn(t, i):
                    n = IMG * (TILES * g + t) + i
                    act.wait_ge(turned, n + 1 + AHEAD)
                    act.wait_ge(q_done, n - 1 + AHEAD)
                    act.copy(onehot_t[:, i % 2, :], PP[2 + i % 2][:, :]).then_inc(turned_sb, 1)

                def out_q(t):
                    act.wait_ge(q_done, IMG * (TILES * g + t + 1) + AHEAD)
                    act.copy(q2[:, bass.ds(128 * t, 128)], P4[:, 0:128]).then_inc(q_sb, 1)

                stage(0, 0)
                stage(0, 1)

                def body(t, last):
                    for i in range(IMG):
                        if i + 2 < IMG:
                            stage(t, i + 2)
                        elif not last:
                            stage(t + 1, i + 2 - IMG)
                        turn(t, i)
                    out_q(t)
                with act.Fori(0, TILES - 1) as t:
                    body(t, False)
                body(TILES - 1, True)

            def cells_copy(g, i):
                n = IMG * g + i
                for b in range(3):
                    act.wait_ge(cells_t, n + 1)
                    if b == 0:
                        if i > 0:
                            act.wait_ge(tabled[i - 1], 16 * (g + 1))
                        else:
                            act.wait_ge(tabled[IMG - 1], 16 * g)
                    m = 512 if b < 2 else 128
                    act.copy(cells[:, 512 * b:512 * b + m], PP[1 + b][:, 0:m]).then_inc(cells_sb, 1)

            def front2(g):
                root(g, 3)
                act.wait_ge(xn3_ready, g + 1)
                act.copy(xn2[:].rearrange("p (h w) -> p h w", w=W),
                         xp3[:, 0:G1 * G1].rearrange("p (h w) -> p h w", w=G1)[:, 1:H + 1, 1:W + 1]
                         ).then_inc(flat3_ready, 1)
                for i in range(IMG - 1):
                    cells_copy(g, i)

            def late(g):
                cells_copy(g, IMG - 1)

            def back(g, i, stage):
                with act.Fori(0, TILES // 2) as p:
                    n = TILES // 2 * (IMG * g + i) + p
                    act.wait_ge(samp_turned, 2 * n + 2 + AHEAD)
                    act.wait_ge(conv3_done, n + AHEAD)
                    act.copy(samp_t[:, 0:2, :], PT[:, :].rearrange("p (r n) -> p r n", r=2)).then_inc(samp_sb, 1)
                    act.copy(samp_t[0:C, 2, :], PT2[0:C, 0:256]).then_inc(samp_sb, 1)

            schedule(act, [front0, front1, front2], late, back)

        @block.vector
        def _(dve):
            def norm(g, n, src, dst):
                for h in range(2):
                    dve.bn_stats(stats[:, h, :], src[:, h * 512:(h + 1) * 512])
                dve.drain()
                dve.bn_aggr(mv[:], stats[:])
                dve.drain()
                dve.tensor_scalar(ve[:], mv[:, 1:2], EPS, None, ALU.add).then_inc(var_ready, 1)
                dve.wait_ge(sd_ready, 4 * g + n + 1)
                dve.reciprocal(nr[:, 0:1], sd[:])
                dve.drain()
                dve.tensor_tensor(nr[:, 1:2], ve[:], nr[:, 0:1], ALU.mult)
                dve.drain()
                dve.tensor_scalar(nr[:, 2:3], nr[:, 1:2], sd[:], 0.5, ALU.add, ALU.mult)
                dve.drain()
                dve.reciprocal(nr[:, 3:4], nr[:, 2:3])
                dve.drain()
                return dve.tensor_scalar(dst, src if len(dst.shape) == 2 else src.rearrange("p (h w) -> p h w", w=W),
                                         mv[:, 0:1], nr[:, 3:4], ALU.subtract, ALU.mult)

            dve.sem_inc(onehot_ready, AHEAD)
            dve.sem_inc(fin_ready, AHEAD)
            for t in (wgrid, xp0, xp1, xp3, bd1):
                dve.memset(t[:], 0.0)
            dve.memset(xs2[C:C + 1, :, :], 1.0)
            dve.memset(negone[:], -1.0)
            dve.drain()
            dve.sem_inc(zeroed, 1)
            dve.wait_ge(loaded, LOADS)
            dve.tensor_tensor(cbsq[:], cb2[0:C, :], cb2[0:C, :], ALU.mult).then_inc(sq_ready, 1)
            dve.wait_ge(norms_ready, 1)
            dve.tensor_copy(cb2[C:C + 1, :], P0[C:C + 1, :])
            dve.tensor_scalar(cb2[0:C, :], cb2[0:C, :], 2.0, None, ALU.mult)

            def front0(g):
                dve.wait_ge(x_loaded, 16 * (g + 1))
                grid0 = xp0[:].rearrange("p (h w) -> p h w", w=G0)
                norm(g, 0, xres[:], grid0[:, 1:H + 1, 1:W + 1])
                dve.drain()
                for v in range(NV):
                    a = grid0[:, PS * v:PS * v + WIN, :]
                    dve.tensor_copy(win[:, NV * v:NV * (v + 1), 0:WIN * WIN].rearrange("p n (r q) -> p n r q", q=WIN),
                                    bass.AP(a.tensor, a.offset, [a.ap[0], [PS, NV], [G0, WIN], [1, WIN]]))
                a = xp0[:]
                dve.tensor_reduce(rowsum[:], bass.AP(a.tensor, a.offset, [a.ap[0], [G0, G0], [PS, NV], [1, WIN]]),
                                  AX.X, ALU.add)
                dve.drain()
                a = rowsum[:]
                dve.tensor_reduce(win[:, :, WIN * WIN].rearrange("p (v h) -> p v h", h=NV),
                                  bass.AP(a.tensor, a.offset, [a.ap[0], [PS * NV, NV], [1, NV], [NV, WIN]]),
                                  AX.X, ALU.add)
                dve.drain()
                dve.tensor_scalar(win[:, :, WIN * WIN], win[:, :, WIN * WIN], 1.0 / (WIN * WIN), None, ALU.mult
                                  ).then_inc(win_ready, 1)
                dve.wait_ge(logit_ready, g + 1)
                dve.tensor_tensor(lg[:, 0], P0[0:PATCHES, 0:IMG * E0].rearrange("p (i e) -> p i e", i=IMG),
                                  bg[:], ALU.add)
                dve.drain()
                dve.tensor_reduce(mx[:, 0], lg[:, 0], AX.X, ALU.max)
                dve.drain()

                def per_image(t):
                    return t.unsqueeze(2).broadcast_to([PATCHES, IMG, E0])
                dve.tensor_tensor(lg[:, 1], lg[:, 0], per_image(mx[:, 0]), ALU.subtract).then_inc(diff_ready, 1)
                dve.tensor_tensor(lg[:, 3], lg[:, 0], per_image(mx[:, 0]), ALU.is_equal)
                dve.drain()
                dve.tensor_tensor(lg[:, 3], lg[:, 3], rank[:], ALU.mult)
                dve.drain()
                dve.tensor_reduce(mx[:, 1], lg[:, 3], AX.X, ALU.max)
                dve.drain()
                dve.tensor_tensor(lg[:, 4], lg[:, 3], per_image(mx[:, 1]), ALU.is_equal)
                dve.wait_ge(exp_ready, g + 1)
                dve.tensor_reduce(mx[:, 2], lg[:, 2], AX.X, ALU.add)
                dve.drain()
                dve.reciprocal(mx[:, 1], mx[:, 2])
                dve.drain()
                dve.tensor_tensor(lg[:, 5], lg[:, 4], per_image(mx[:, 1]), ALU.mult).then_inc(route_ready, 1)
                dve.wait_ge(route_t, g + 1)
                dve.tensor_copy(rt_t[:], P0[0:IMG * E0, 64:64 + PATCHES]).then_inc(route_t_sb, 1)
                dve.wait_ge(route_b, g + 1)
                dve.tensor_copy(rtb[:], P1[:, 0:2 * IMG * PATCHES].rearrange("p (k n) -> p k n", n=PATCHES)
                                ).then_inc(route_ready, 1)
                dve.drain()
                with dve.Fori(0, NV) as v:
                    for i in range(IMG):
                        n = IMG * (NV * g + v) + i
                        dve.wait_ge(relu_done, 2 * (n + 1) + AHEAD)
                        e = ex0[:, i % 2].rearrange("p h (n s) -> p h n s", s=PS * PS)
                        r = rtb[:, 2 * i:2 * i + 2, bass.ds(NV * v, NV)].unsqueeze(3)
                        dve.tensor_tensor(e, e, r.broadcast_to([128, 2, NV, PS * PS]), ALU.mult
                                          ).then_inc(gated, 1)
                dve.wait_ge(y_in, 16 * (g + 1))
                for v in range(H // PS):
                    x = xres[:, PS * W * v:PS * W * (v + 1)].rearrange("p (r h q) -> p r h q", r=PS, q=PS)
                    y = yb[:, ROWN * v:ROWN * v + PS * PS * (W // PS)].rearrange("p (h r q) -> p r h q", r=PS, q=PS)
                    dve.tensor_tensor(x, x, y, ALU.add)
                dve.drain()

            def front1(g):
                dve.wait_ge(off_done, g)
                grid1 = xp1[:].rearrange("p (h w) -> p h w", w=G1)[:, 1:H + 1, 1:W + 1]
                norm(g, 1, xres[:], grid1)
                dve.drain()
                dve.tensor_reduce(sm1[:, 0, 0:1], grid1, AX.XY, ALU.add)
                dve.drain()
                dve.tensor_scalar(sm1[:, 3, :], wroute[:], sm1[:, 0, 0:1], 1.0 / PIX, ALU.mult, ALU.mult
                                  ).then_inc(pooled, 1)
                dve.wait_ge(rlog_ready, g + 1)
                dve.tensor_tensor(sm1[:, 1, :], P0[:, 0:E1], broute[:], ALU.add).then_inc(z_ready, 1)
                dve.wait_ge(ez_ready, g + 1)
                dve.tensor_scalar(sm1[:, 2, :], sm1[:, 2, :], 1.0, None, ALU.add)
                dve.drain()
                dve.reciprocal(sm1[:, 0, :], sm1[:, 2, :])
                dve.drain()
                dve.tensor_scalar(mix[:], wmix[:, 0, :], sm1[:, 0, 0:1], None, ALU.mult)
                for e in range(1, E1):
                    dve.drain()
                    dve.scalar_tensor_tensor(out=mix[:], in0=wmix[:, e, :], scalar=sm1[:, 0, e:e + 1], in1=mix[:],
                                             op0=ALU.mult, op1=ALU.add)
                dve.drain()
                for i in range(IMG):
                    r = slice(C * i, C * (i + 1))
                    dve.tensor_copy(bd1[r, :, r], mix[r, :].rearrange("p (k o) -> p k o", o=C)).then_inc(bd_ready, 1)
                for h in range(2):
                    dve.wait_ge(conv1_done, 2 * g + h + 1)
                    x = xres[:, 512 * h:512 * (h + 1)]
                    dve.tensor_tensor(x, x, PP[1 + h][:, :], ALU.add).then_inc(x2_ready, 1)
                dve.drain()
                norm(g, 2, xres[:], xn2[:]).then_inc(xn2_ready, 1)

                def unit(t, i):
                    n = IMG * (TILES * g + t) + i
                    dve.wait_ge(score_done, n + 1 + AHEAD)
                    dve.sem_inc(dve_passed, 1)
                    dve.max(top[:, i % 2, :], PP[i % 2][:, :])
                    dve.drain()
                    dve.max_index(code[:, i % 2, :], top[:, i % 2, :], PP[i % 2][:, :])
                    dve.drain()
                    dve.wait_ge(turned, n - 1 + AHEAD)
                    dve.tensor_scalar(onehot[:, i % 2, :], iota[:], code[:, i % 2, 0:1], None, ALU.is_equal
                                      ).then_inc(onehot_ready, 1)
                with dve.Fori(0, TILES) as t:
                    for i in range(IMG):
                        unit(t, i)

            def front2(g):
                dve.wait_ge(q_sb, TILES * (g + 1) + AHEAD)
                dve.tensor_tensor(q2[:], q2[:], xn2[:], ALU.subtract)
                dve.tensor_copy(xlast[P - C:P, :], xfin[P - C:P, :]) if not isinstance(g, int) else None
                dve.drain()
                dve.tensor_tensor(q2[:], q2[:], xn2[:], ALU.add)
                dve.drain()
                dve.tensor_tensor(xfin[:], xres[:], q2[:], ALU.add).then_inc(x3_ready, 1)
                dve.drain()
                dve.wait_ge(xs3_loaded, 16 * CORN * IMG * g)
                norm(g, 3, xfin[:], xp3[:, 0:G1 * G1].rearrange("p (h w) -> p h w", w=G1)[:, 1:H + 1, 1:W + 1]
                     ).then_inc(xn3_ready, 1)
                dve.wait_ge(off_done, g + 1)
                ht = TILES // 2
                for h in range(2):
                    for a in range(2):
                        src = PP[h][:, 0:ht * IMG * 2 * TAPS].rearrange(
                            "p (t i k a) -> p a i t k", t=ht, i=IMG, a=2)[:, a]
                        dst = pos[:, a].rearrange("p i (t k) -> p i t k", k=TAPS)[:, :, ht * h:ht * (h + 1), :]
                        b = bgrid[:].rearrange("p (k a) -> p a k", a=2)[:, a].unsqueeze(1).unsqueeze(1)
                        dve.tensor_tensor(dst, src, b.broadcast_to([128, IMG, ht, TAPS]), ALU.add
                                          ).then_inc(off_read, 1)
                dve.drain()
                for a in range(2):
                    dve.tensor_tensor(pos[:, a], pos[:, a],
                                      grid[:, a:a + 1, :].broadcast_to([128, IMG, TILES * TAPS]), ALU.add)
                dve.drain()
                p = pos[:].rearrange("p a i n -> p (a i n)")
                f = cell[:].rearrange("p a n -> p (a n)")
                o = over[:].rearrange("p a n -> p (a n)")
                dve.tensor_scalar(p, p, 1.0, 0.5, ALU.add, ALU.mult)
                dve.drain()
                dve.tensor_scalar(p, p, float(W - 1), -1.0, ALU.mult, ALU.max)
                dve.drain()
                dve.tensor_scalar(p, p, float(W), None, ALU.min)
                dve.drain()
                dve.tensor_copy(cell_i[:], p)
                dve.drain()
                dve.tensor_copy(f, cell_i[:])
                dve.drain()
                dve.tensor_tensor(o, f, p, ALU.is_gt)
                dve.drain()
                dve.tensor_tensor(f, f, o, ALU.subtract)
                dve.drain()
                dve.tensor_scalar(f, f, float(W - 1), None, ALU.min)
                dve.drain()
                dve.tensor_tensor(p, p, f, ALU.subtract)
                dve.scalar_tensor_tensor(out=idx[:].rearrange("p i t k -> p (i t k)"), in0=cell[:, 1],
                                         scalar=float(G1), in1=cell[:, 0], op0=ALU.mult, op1=ALU.add)
                dve.drain()
                dve.tensor_scalar(o, p, -1.0, 1.0, ALU.mult, ALU.add)
                dve.drain()
                far = pos[:].rearrange("p a i n -> p a (i n)")
                for q in range(CORN):
                    wy = (far if q // 2 else over)[:, 1]
                    wx = (far if q % 2 else over)[:, 0]
                    dve.tensor_tensor(wq[:].rearrange("p i t (k q) -> p (i t k) q", q=CORN)[:, :, q], wx, wy, ALU.mult)
                dve.drain()
                if isinstance(g, int):
                    for t in range(TILES):
                        stage_slot(0, t)

            def stage_slot(i, t):
                dve.tensor_copy(w_slot[:, t, :], wq[:, i, t, :])
                dve.tensor_scalar(idx_slot[:, t, :], idx[:, i, t, :], float(G1 + 1), None, ALU.add
                                  ).then_inc(granted, 1)

            def late(g):
                pass

            def back(g, i, stage):
                def residual(p):
                    n = TILES // 2 * (IMG * g + i) + p
                    dve.wait_ge(conv3_done, n + 1 + AHEAD)
                    if p == 0:
                        dve.wait_ge(stored, 16 * (IMG * (g - 1) + i + 1) + STORED_AHEAD)
                    src = xlast if i == IMG - 1 and not (isinstance(g, int)) else xfin
                    r = slice(C * i, C * (i + 1))
                    c = slice(256 * p, 256 * (p + 1))
                    dve.tensor_tensor(fin[r, c], src[r, c], PO[r, 0:256], ALU.add).then_inc(fin_ready, 1)

                for t in range(TILES):
                    n = TILES * (IMG * g + i) + t
                    dve.wait_ge(gathered[t], 16 * TAPS * (IMG * g + i + 1))
                    s = ring[:, t, :].rearrange("p (n c) -> p n c", c=C)
                    w = w_slot[:, t, :].unsqueeze(2).broadcast_to([128, TAPS * CORN, C])
                    dve.tensor_tensor(s, s, w, ALU.mult)
                    dve.drain()
                    s = ring[:, t, :].rearrange("p (k y n) -> p k y n", k=TAPS, y=2)
                    dve.tensor_tensor(pair[:].rearrange("p k x c -> p k (x c)"), s[:, :, 0], s[:, :, 1], ALU.add)
                    dve.drain()
                    if stage:
                        stage_slot((i + 1) % IMG, t)
                    dve.wait_ge(samp_turned, n - 1 + AHEAD)
                    dve.tensor_tensor(samp[:, t % 2, :].rearrange("p (k c) -> p k c", c=C), pair[:, :, 0], pair[:, :, 1],
                                      ALU.add).then_inc(samp_ready, 1)
                    dve.drain()
                    if t % 2 and t > 1:
                        residual(t // 2 - 1)
                residual(TILES // 2 - 1)

            schedule(dve, [front0, front1, front2], late, back)

        @block.tensor
        def _(pe):
            pe.sem_inc(sum0_done, AHEAD)
            pe.sem_inc(score_done, AHEAD)
            pe.sem_inc(q_done, AHEAD)
            pe.sem_inc(turned, AHEAD)
            pe.sem_inc(samp_turned, AHEAD)
            pe.sem_inc(conv3_done, AHEAD)
            pe.wait_ge(sq_ready, 1)
            pe.matmul(P0[C:C + 1, :], negone[:], cbsq[:], start=True, stop=True).then_inc(norms_ready, 1)

            def front0(g):
                pe.wait_ge(xs0_loaded, 16 * 3 * IMG * (g + 1))
                pe.sem_inc(pe_passed, 1)
                for i in range(IMG):
                    m = pe.matmul(P0[0:PATCHES, E0 * i:E0 * (i + 1)], xs0[2 * C:3 * C, i, :, CUT - 1],
                                  wg[2 * C:3 * C, :], start=True, stop=True)
                m.then_inc(logit_ready, 1)
                pe.wait_ge(route_ready, 2 * g + 1)
                pe.sem_inc(pe_passed, 1)
                pe.transpose(P0[0:IMG * E0, 64:64 + PATCHES], lg[:, 5].rearrange("p i e -> p (i e)"),
                             ident[0:PATCHES, 0:PATCHES]).then_inc(route_t, 1)
                pe.wait_ge(route_t_sb, g + 1)
                pe.wait_ge(cells_sb, 3 * IMG * g)
                for k in range(2 * IMG):
                    m = pe.matmul(P1[:, PATCHES * k:PATCHES * (k + 1)], pick[:, k, :], rt_t[:], start=True, stop=True)
                m.then_inc(route_b, 1)
                pe.wait_ge(route_ready, 2 * g + 2)
                pe.sem_inc(pe_passed, 1)

                def conv(v, i):
                    n = IMG * (NV * g + v) + i
                    pe.wait_ge(relu_done, 2 * (n - 1) + AHEAD)
                    for h in range(2):
                        for dx in range(3):
                            a = xs0[:, i, bass.ds(NV * v, NV), dx:CUT - 1]
                            a = bass.AP(a.tensor, a.offset, [a.ap[0], [CUT, NV], [WIN, PS], [1, PS]])
                            m = pe.matmul(PP[2 * (i % 2) + h][:, 0:ROWN], w0[:, dx, h, :], a,
                                          start=(dx == 0), stop=(dx == 2))
                        m.then_inc(conv0_done, 1)

                def add_up(v, i):
                    n = IMG * (NV * g + v) + i
                    pe.wait_ge(gated, n + 1)
                    if i == 0:
                        pe.wait_ge(yc_done, NV * g + v + AHEAD)
                    for h in range(2):
                        m = pe.matmul(P4[C * i:C * (i + 1), 0:ROWN], sume[:], ex0[:, i % 2, h, :],
                                      start=(h == 0), stop=(h == 1))
                    m.then_inc(sum0_done, 1)
                with pe.Fori(0, NV) as v:
                    for i in range(IMG):
                        conv(v, i)
                        if i:
                            add_up(v, i - 1)
                    add_up(v, IMG - 1)

            def front1(g):
                pe.wait_ge(pooled, g + 1)
                pe.matmul(P0[:, 0:E1], same[:], sm1[:, 3, :], start=True, stop=True).then_inc(rlog_ready, 1)
                pe.wait_ge(bd_ready, IMG * (g + 1))
                grid1 = xp1[:].rearrange("p (h w) -> p h w", w=G1)
                for h in range(2):
                    for k in range(TAPS):
                        y = H // 2 * h + k // 3
                        m = pe.matmul(PP[1 + h][:, :], bd1[:, k, :], grid1[:, y:y + H // 2, k % 3:k % 3 + W],
                                      start=(k == 0), stop=(k == TAPS - 1))
                    m.then_inc(conv1_done, 1)
                pe.wait_ge(x2_ready, 2 * (g + 1))

                def scores(t, i):
                    n = IMG * (TILES * g + t) + i
                    pe.wait_ge(staged2, n + 1)
                    pe.wait_ge(onehot_ready, n - 1 + AHEAD)
                    pe.matmul(PP[i % 2][:, :], xs2[:, i % 2, :], cb2[:], start=True, stop=True).then_inc(score_done, 1)

                def turn(t, i):
                    n = IMG * (TILES * g + t) + i
                    pe.wait_ge(onehot_ready, n + 1 + AHEAD)
                    pe.wait_ge(turned_sb, n - 1 + AHEAD)
                    for c in range(CCH):
                        m = pe.transpose(PP[2 + i % 2][:, 128 * c:128 * (c + 1)],
                                         onehot[:, i % 2, 128 * c:128 * (c + 1)], ident[:])
                    m.then_inc(turned, 1)

                def pick_code(t, i):
                    n = IMG * (TILES * g + t) + i
                    pe.wait_ge(turned_sb, n + 1 + AHEAD)
                    if i == 0:
                        pe.wait_ge(q_sb, TILES * g + t + AHEAD)
                    for c in range(CCH):
                        m = pe.matmul(P4[C * i:C * (i + 1), 0:128], codes[:, c, :],
                                      onehot_t[:, i % 2, 128 * c:128 * (c + 1)],
                                      start=(c == 0), stop=(c == CCH - 1))
                    m.then_inc(q_done, 1)

                def body(t, first):
                    for i in range(IMG):
                        scores(t, i)
                        if i > 0 or not first:
                            turn(t if i else t - 1, (i - 1) % IMG)
                        if i > 1 or not first:
                            pick_code(t if i > 1 else t - 1, (i - 2) % IMG)
                body(0, True)
                with pe.Fori(1, TILES) as t:
                    body(t, False)
                turn(TILES - 1, IMG - 1)
                pick_code(TILES - 1, IMG - 2)
                pick_code(TILES - 1, IMG - 1)

            def table_t(g, i):
                n = IMG * g + i
                pe.wait_ge(xs3_loaded, 16 * CORN * (n + 1))
                if i == 0:
                    pe.wait_ge(off_read, 4 * (g + 1))
                pe.wait_ge(cells_sb, 3 * n)
                for c in range(TROWS // 128):
                    m = pe.transpose(PP[1 + c // 4][:, 128 * (c % 4):128 * (c % 4 + 1)],
                                     xs3[:, i % 2, 128 * c:128 * (c + 1)], ident[:])
                m.then_inc(cells_t, 1)

            def front2(g):
                pe.wait_ge(flat3_ready, g + 1)
                ht = TILES // 2
                for t in range(TILES):
                    n = IMG * 2 * TAPS
                    m = pe.matmul(PP[t // ht][:, n * (t % ht):n * (t % ht + 1)],
                                  xn2[:, 128 * t:128 * (t + 1)], wgrid[:], start=True, stop=True)
                m.then_inc(off_done, 1)
                for i in range(IMG - 1):
                    table_t(g, i)

            def late(g):
                table_t(g, IMG - 1)

            def back(g, i, stage):
                with pe.Fori(0, TILES // 2) as p:
                    n = TILES // 2 * (IMG * g + i) + p
                    for j in range(2):
                        pe.wait_ge(samp_ready, 2 * n + j + 1)
                        if j == 0:
                            pe.wait_ge(samp_sb, 2 * n + AHEAD)
                        for r in range(2):
                            pe.transpose(PT[:, 256 * r + 128 * j:256 * r + 128 * (j + 1)],
                                         samp[:, j, 128 * r:128 * (r + 1)], ident[:])
                        pe.transpose(PT2[0:C, 128 * j:128 * (j + 1)], samp[:, j, 256:TC], ident[:]
                                     ).then_inc(samp_turned, 1)
                    pe.wait_ge(samp_sb, 2 * (n + 1) + AHEAD)
                    pe.wait_ge(fin_ready, n + AHEAD)
                    for r in range(3):
                        k = min(128, TC - 128 * r)
                        m = pe.matmul(PO[C * i:C * (i + 1), 0:256], wc[0:k, r, :], samp_t[0:k, r, :],
                                      start=(r == 0), stop=(r == 2))
                    m.then_inc(conv3_done, 1)

            schedule(pe, [front0, front1, front2], late, back)


LOADS = 16 * (10 + IMG + 2 * IMG + 5 + 3)


def constants():
    f = np.float32
    pick = np.zeros((IMG * E0, 2 * IMG, 128), f)
    for i in range(IMG):
        for e in range(E0):
            pick[i * E0 + e, 2 * i + e // HALF, (e % HALF) * C:(e % HALF + 1) * C] = 1
    grid = np.zeros((128, 2, TILES, TAPS), f)
    base = np.linspace(-1.0, 1.0, W, dtype=f)
    koff = np.linspace(-2 / (W - 1), 2 / (W - 1), 3, dtype=f)
    for t in range(TILES):
        for p in range(128):
            y, x = divmod(128 * t + p, W)
            for k in range(TAPS):
                grid[p, 0, t, k] = base[x] + koff[k % 3]
                grid[p, 1, t, k] = base[y] + koff[k // 3]
    return {
        "ident": np.eye(128, dtype=f),
        "pick_expert": pick,
        "sum_experts": np.tile(np.eye(C, dtype=f), (HALF, 1)),
        "same_image": np.kron(np.eye(IMG, dtype=f), np.ones((C, C), f)),
        "code_iota": np.tile(np.arange(CODES, dtype=f), (128, 1)),
        "first_rank": np.tile(np.arange(E0, 0, -1, dtype=f), (PATCHES, IMG, 1)),
        "grid": grid.reshape(128, 2, TILES * TAPS),
    }


def kernel(**inputs):
    import concourse.bacc as bacc
    from concourse.bass_utils import run_bass_kernel_spmd

    a = {k: np.asarray(v) for k, v in inputs.items()}
    arrays = {
        "x": a["x"].reshape(B * C, PIX),
        "Wg": a["L0_conv_Wg"],
        "bg": np.broadcast_to(a["L0_conv_bg"], (IMG, E0)),
        "Wexp": a["L0_conv_Wexp"].transpose(3, 2, 4, 0, 1).reshape(3 * C, 3, 2, HALF * C),
        "bexp": a["L0_conv_bexp"].reshape(2, HALF * C).T,
        "w_route": a["L1_conv_w_route"].T,
        "b_route": a["L1_conv_b_route"],
        "w_mix": a["L1_conv_w_experts"].transpose(2, 0, 3, 4, 1).reshape(C, E1, TC),
        "codebook": a["L2_conv_codebook"],
        "codebook_t": a["L2_conv_codebook"].T,
        "w_grid": a["L3_conv_w_grid"].T,
        "b_grid": a["L3_conv_b_grid"],
        "w_conv": a["L3_conv_w_conv"].transpose(2, 3, 1, 0).reshape(TC, C),
    }
    arrays.update(constants())
    arrays = {f"in_{k}": np.ascontiguousarray(v) for k, v in arrays.items()}
    nc = bacc.Bacc("TRN2", target_bir_lowering=False, num_devices=1)
    aps = {k: nc.dram_tensor(f"in_{k}", arrays[f"in_{k}"].shape, mybir.dt.from_np(arrays[f"in_{k}"].dtype),
                             kind="ExternalInput").ap() for k in INPUTS}
    aps["out"] = nc.dram_tensor("out", (B * C, PIX), F32, kind="ExternalOutput").ap()
    build(nc, aps, aps["out"])
    r = run_bass_kernel_spmd(nc, [arrays], core_ids=[0])
    return r.results[0]["out"].reshape(B, C, H, W)
```

```python
from contextlib import ExitStack

import numpy as np

import concourse.bass as bass
from concourse import mybir

ALU = mybir.AluOpType
ACT = mybir.ActivationFunctionType
AX = mybir.AxisListType
F32 = mybir.dt.float32
I32 = mybir.dt.int32
U32 = mybir.dt.uint32
BF16 = mybir.dt.bfloat16
F16 = mybir.dt.float16

B, C, H, W = 32, 32, 32, 32
PIX = H * W
IMG = 4
GROUPS = B // IMG
P = IMG * C
PS = 8
NV = H // PS + 1
PATCHES = NV * NV
WIN = PS + 2
G0 = NV * PS + 2
WROW = WIN * WIN + 1
CUT = PS * WIN + 1
E0 = 8
HALF = 4
ROWN = NV * PS * PS
E1 = 4
G1 = W + 2
TAPS = 9
CODES = 512
CCH = CODES // 128
TILES = PIX // 128
CORN = 4
TROWS = 9 * 128
XP3 = TROWS + G1 + 2
ROW = TAPS * CORN * C
TC = TAPS * C
EPS = 1e-5
AHEAD = 3
STORED_AHEAD = 16 * (IMG + 1)
PARTS = 3

INPUTS = ["x", "Wg", "bg", "Wexp", "bexp", "w_route", "b_route", "w_mix", "codebook", "codebook_t",
          "w_grid", "b_grid", "w_conv", "ident", "pick_expert", "sum_experts", "same_image",
          "code_iota", "first_rank", "grid"]


def build(nc, A, out):
    ctx = ExitStack()
    with ctx:
        def sb(name, shape, dt=F32):
            return ctx.enter_context(nc.sbuf_tensor(name, shape, dt))

        def bank(name):
            return ctx.enter_context(nc.psum_tensor(name, [128, 512], F32))

        def sem(name):
            return ctx.enter_context(nc.semaphore(name))

        ident = sb("ident_sb", [128, 128])
        pick = sb("pick_sb", [IMG * E0, 2 * IMG, 128])
        sume = sb("sume_sb", [128, C])
        same = sb("same_sb", [128, 128])
        iota = sb("iota_sb", [128, CODES], F16)
        rank = sb("rank_sb", [PATCHES, IMG, E0])
        grid = sb("grid_sb", [128, 2, TILES * TAPS])
        w0 = sb("w0", [3 * C, 3, 2, 128])
        bexp = sb("bexp_sb", [128, 2])
        wg = sb("wg_sb", [3 * C, E0])
        bg = sb("bg_sb", [PATCHES, IMG, E0])
        wmix = sb("wmix", [128, E1, TC])
        wroute = sb("wroute", [128, E1])
        broute = sb("broute", [128, E1])
        cb2 = sb("cb2", [128, CODES])
        negone = sb("negone", [C, 1])
        codes = sb("codes", [128, CCH * C])
        codes_b = sb("codes_b", [128, PARTS, CCH * C], BF16)
        wgrid = sb("wgrid", [128, IMG * 2 * TAPS])
        bgrid = sb("bgrid", [128, 2 * TAPS])
        wc = sb("wc", [128, 3, C])
        xres = sb("xres", [128, PIX])
        xfin = sb("xfin", [128, PIX])
        xlast = sb("xlast", [128, PIX])
        stats = sb("stats", [128, 2, 6])
        mv = sb("mv", [128, 2])
        ve = sb("ve", [128, 1])
        sd = sb("sd", [128, 1])
        nr = sb("nr", [128, 4])
        xp0 = sb("xp0", [128, G0 * G0])
        arena = sb("arena", [128, IMG * PATCHES * CUT])
        xs0 = arena[0:3 * C, :].rearrange("p (i n s) -> p i n s", i=IMG, s=CUT)
        xs3 = arena[:, 0:2 * TROWS].rearrange("p (b n) -> p b n", b=2)
        cells = arena[:, 2 * TROWS:3 * TROWS]
        cbsq = arena[0:C, 0:CODES]
        iota_f = arena[:, CODES:2 * CODES]
        qx = arena[:, 0:PIX].rearrange("p (t c) -> p t c", c=128)
        codes_rest = arena[:, 2 * CODES:2 * CODES + CCH * C]
        rowsum = sb("rowsum", [128, G0, NV])
        lg = sb("lg", [PATCHES, 6, IMG, E0])
        mx = sb("mx", [PATCHES, 3, IMG])
        rt_t = sb("rt_t", [IMG * E0, PATCHES])
        rtb = sb("rtb", [128, 2 * IMG, PATCHES])
        ex0 = sb("ex0", [128, 2, 2, ROWN])
        blocks = sb("blocks", [128, 2 * NV * ROWN])
        win = blocks[:, 0:PATCHES * WROW].rearrange("p (n s) -> p n s", s=WROW)
        yc = blocks[:, 0:NV * ROWN]
        yb = blocks[:, NV * ROWN:2 * NV * ROWN]
        xp1 = sb("xp1", [128, G1 * G1])
        sm1 = sb("sm1", [128, 4, E1])
        mix = sb("mix", [128, TC])
        bd1 = sb("bd1", [128, TAPS, 128])
        xn2 = sb("xn2", [128, PIX])
        xs2 = sb("xs2", [128, IMG, 128])
        onehot = sb("onehot", [128, 2, CODES], BF16)
        onehot_t = sb("onehot_t", [128, 2, CODES], BF16)
        ident_b = sb("ident_b", [128, 128], BF16)
        top = sb("top", [128, 2, 8])
        code = sb("code", [128, 2, 8], U32)
        q2 = sb("q2", [128, PIX])
        xp3 = sb("xp3", [128, XP3])
        NK = IMG * TILES * TAPS
        pos = sb("pos", [128, 2, IMG, TILES * TAPS])
        cell_i = sb("cell_i", [128, 2 * NK], I32)
        cell = sb("cell", [128, 2, NK])
        over = sb("over", [128, 2, NK])
        idx = sb("idx_sb", [128, IMG, TILES, TAPS])
        wq = sb("wq", [128, IMG, TILES, TAPS * CORN])
        idx_slot = sb("idx_slot", [128, TILES, TAPS], U32)
        w_slot = sb("w_slot", [128, TILES, TAPS * CORN])
        ring = sb("ring", [128, TILES, ROW])
        pair = sb("pair", [128, TAPS, 2, C])
        samp = sb("samp", [128, TC])
        samp_t = sb("samp_t", [128, 3, 128])
        fin = sb("fin", [128, PIX])

        P0, P1, P2, P3, P4, P5, PT, PO = [bank(f"bank{n}") for n in range(8)]
        PP = [P0, P1, P2, P3, P4]
        SCORES = [P0, P1, P3, P5]

        win_dram = nc.dram_tensor("windows", [IMG, C * PATCHES, WROW], F32).ap()
        y_dram = nc.dram_tensor("y_patches", [IMG, C * PATCHES, PS * PS], F32).ap()
        table = [nc.dram_tensor(f"cells_{i}", [TROWS, CORN * C], F32).ap() for i in range(IMG)]

        loaded = sem("loaded")
        zeroed = sem("zeroed")
        sq_ready = sem("sq_ready")
        norms_ready = sem("norms_ready")
        x_loaded = sem("x_loaded")
        x3_ready = sem("x3_ready")
        var_ready = sem("var_ready")
        sd_ready = sem("sd_ready")
        win_ready = sem("win_ready")
        win_out = sem("win_out")
        xs0_loaded = sem("xs0_loaded")
        logit_ready = sem("logit_ready")
        diff_ready = sem("diff_ready")
        exp_ready = sem("exp_ready")
        route_ready = sem("route_ready")
        route_t = sem("route_t")
        route_t_sb = sem("route_t_sb")
        route_b = sem("route_b")
        conv0_done = sem("conv0_done")
        relu_done = sem("relu_done")
        gated = sem("gated")
        sum0_done = sem("sum0_done")
        yc_done = sem("yc_done")
        y_out = sem("y_out")
        y_in = sem("y_in")
        pooled = sem("pooled")
        rlog_ready = sem("rlog_ready")
        z_ready = sem("z_ready")
        ez_ready = sem("ez_ready")
        bd_ready = sem("bd_ready")
        conv1_done = sem("conv1_done")
        x2_ready = sem("x2_ready")
        xn2_ready = sem("xn2_ready")
        staged2 = sem("staged2")
        score_done = sem("score_done")
        onehot_ready = sem("onehot_ready")
        turned = sem("turned")
        turned_sb = sem("turned_sb")
        q_done = sem("q_done")
        qx_ready = sem("qx_ready")
        qx_turned = sem("qx_turned")
        xn3_ready = sem("xn3_ready")
        flat3_ready = sem("flat3_ready")
        off_done = sem("off_done")
        xs3_loaded = [sem("xs3_loaded_even"), sem("xs3_loaded_odd")]
        cells_t = sem("cells_t")
        cells_sb = sem("cells_sb")
        tabled = [sem(f"tabled{i}") for i in range(IMG)]
        granted = sem("granted")
        gathered = [sem("gathered_even"), sem("gathered_odd")]
        tile_ready = sem("tile_ready")
        samp_ready = sem("samp_ready")
        samp_turned = sem("samp_turned")
        samp_sb = sem("samp_sb")
        conv3_done = sem("conv3_done")
        fin_ready = sem("fin_ready")
        stored = sem("stored")

        pe_passed, dve_passed = sem("pe_passed"), sem("dve_passed")
        pool_passed, sp_passed = sem("pool_passed"), sem("sp_passed")

        block = ctx.enter_context(nc.Block())

        def schedule(eng, front, tile, end):
            front(0, lambda *a: None, lambda i: None)
            with eng.Fori(0, GROUPS - 1) as g:
                front(g + 1, lambda i, t, *a: tile(g, i, t, *a), lambda i: end(g, i))
            for i in range(IMG):
                tile(GROUPS - 1, i, 0)
                with eng.Fori(1, TILES) as t:
                    tile(GROUPS - 1, i, t)
                end(GROUPS - 1, i)

        @block.sync
        def _(sp):
            sp.sem_inc(stored, STORED_AHEAD)
            for dst, src in (
                (ident[:], A["ident"]), (pick[:], A["pick_expert"]), (sume[:], A["sum_experts"]),
                (same[:], A["same_image"]), (rank[:], A["first_rank"]), (grid[:], A["grid"]),
                (w0[:], A["Wexp"]), (bexp[:], A["bexp"]), (bg[:], A["bg"].partition_broadcast(PATCHES)),
            ):
                sp.dma_start(dst, src).then_inc(loaded, 16)
            sp.wait_ge(zeroed, 1)
            for i in range(IMG):
                r = slice(C * i, C * (i + 1))
                sp.dma_start(wgrid[r, 2 * TAPS * i:2 * TAPS * (i + 1)], A["w_grid"]).then_inc(loaded, 16)
            sp.dma_start(wg[2 * C:3 * C, :], A["Wg"]).then_inc(loaded, 16)

            def load_x(g):
                sp.wait_ge(x3_ready, g)
                sp.dma_start(xres[:], A["x"].rearrange("(g p) n -> g p n", p=P)[bass.ds(g, 1)]
                             .rearrange("g p n -> (g p) n")).then_inc(x_loaded, 16)

            def front(g, tile, end):
                load_x(g)
                sp.wait_ge(win_ready, g + 1)
                sp.sem_inc(sp_passed, 1)
                sp.wait_ge(xs0_loaded, 16 * 3 * IMG * g)
                sp.sem_inc(sp_passed, 1)
                sp.dma_start(win_dram.rearrange("i (c n) s -> (i c) (n s)", c=C),
                             win.rearrange("p n s -> p (n s)")).then_inc(win_out, 16)
                sp.wait_ge(win_out, 16 * (g + 1))
                sp.sem_inc(sp_passed, 1)
                sp.wait_ge(tabled[IMG - 1], 16 * g)
                sp.sem_inc(sp_passed, 1)
                for i in range(IMG):
                    for dy in range(3):
                        n = CUT if dy == 2 else CUT - 1
                        sp.dma_start(xs0[C * dy:C * (dy + 1), i, :, 0:n],
                                     win_dram[i].rearrange("(p c) s -> c p s", c=C)[:, :, dy * WIN:dy * WIN + n]
                                     ).then_inc(xs0_loaded, 16)
                sp.wait_ge(yc_done, NV * (g + 1) + AHEAD)
                sp.wait_ge(y_in, 16 * g)
                for i in range(IMG):
                    sp.dma_start(y_dram[i].rearrange("(p c) s -> c p s", c=C),
                                 yc[C * i:C * (i + 1), :].rearrange("c (p s) -> c p s", s=PS * PS)
                                 ).then_inc(y_out, 16)
                sp.wait_ge(y_out, 16 * IMG * (g + 1))
                sp.dma_start(yb[:], y_dram.rearrange("i (c n) s -> (i c) (n s)", c=C)).then_inc(y_in, 16)

                end(0)
                end(1)

                def shift(i):
                    if i >= 2:
                        sp.wait_ge(cells_t, IMG * g + i - 1)
                    for q in range(CORN):
                        f = (q // 2) * G1 + q % 2
                        sp.dma_start(xs3[C * q:C * (q + 1), i % 2, :],
                                     xp3[C * i:C * (i + 1), f:f + TROWS]).then_inc(xs3_loaded[i % 2], 16)

                def write_table(i):
                    sp.wait_ge(cells_sb, 3 * (IMG * g + i + 1))
                    sp.sem_inc(sp_passed, 1)
                    if not isinstance(g, int):
                        sp.wait_ge(samp_ready, TILES * (IMG * (g - 1) + i + 1))
                        sp.sem_inc(sp_passed, 1)
                    sp.dma_start(table[i].rearrange("(n p) c -> p n c", p=128),
                                 cells.rearrange("p (n c) -> p n c", c=128)).then_inc(tabled[i], 16)
                sp.wait_ge(xn3_ready, g + 1)
                shift(0)
                shift(1)
                for i in range(IMG):
                    write_table(i)
                    if i + 2 < IMG:
                        shift(i + 2)
                    if i == 0:
                        end(2)
                end(3)

            def tile(g, i, t):
                pass

            def end(g, i):
                sp.wait_ge(fin_ready, TILES * (IMG * g + i + 1) + AHEAD)
                sp.wait_ge(stored, 16 * (IMG * g + i) + STORED_AHEAD)
                rows = A["out"].rearrange("(n p) m -> n p m", p=C)
                sp.dma_start(rows[bass.ds(IMG * g + i, 1)].rearrange("n p m -> (n p) m"),
                             fin[C * i:C * (i + 1), :]).then_inc(stored, 16)

            schedule(sp, front, tile, end)
            sp.wait_ge(stored, 16 * B + STORED_AHEAD)

        @block.gpsimd
        def _(pool):
            def seen(n):
                pool.wait_ge(gathered[n % 2], 16 * TAPS * (TILES * IMG // 2 * g + n // 2 + 1))
                pool.sem_inc(tile_ready, 1)

            with pool.Fori(0, GROUPS) as g:
                for i in range(IMG):
                    pool.wait_ge(tabled[i], 16 * (g + 1))
                    for t in range(TILES):
                        n = TILES * i + t
                        pool.wait_ge(granted, IMG * TILES * g + n + 1)
                        pool.sem_inc(pool_passed, 1)
                        for k in range(TAPS):
                            pool.indirect_dma_start(
                                ring[:, t, CORN * C * k:CORN * C * (k + 1)], None, table[i],
                                bass.IndirectOffsetOnAxis(ap=idx_slot[:, t, k:k + 1], axis=0),
                            ).then_inc(gathered[t % 2], 16)
                        if n > 0:
                            seen(n - 1)
                seen(IMG * TILES - 1)

        @block.scalar
        def _(act):
            for i in range(IMG):
                r = slice(C * i, C * (i + 1))
                act.dma_start(wmix[r], A["w_mix"]).then_inc(loaded, 16)
                act.dma_start(wroute[r], A["w_route"]).then_inc(loaded, 16)
            act.dma_start(broute[:], A["b_route"].partition_broadcast(128)).then_inc(loaded, 16)
            act.dma_start(cb2[0:C, :], A["codebook_t"]).then_inc(loaded, 16)
            act.dma_start(codes[:].rearrange("p (k c) -> p k c", c=C),
                          A["codebook"].rearrange("(k p) c -> p k c", p=128)).then_inc(loaded, 16)
            act.dma_start(iota_f, A["code_iota"]).then_inc(loaded, 16)
            act.dma_start(bgrid[:], A["b_grid"].partition_broadcast(128)).then_inc(loaded, 16)
            for r in range(3):
                n = min(128, TC - 128 * r)
                act.dma_start(wc[0:n, r, :], A["w_conv"][128 * r:128 * r + n, :]).then_inc(loaded, 16)
            act.wait_ge(loaded, LOADS)
            act.sem_inc(relu_done, AHEAD)
            act.sem_inc(turned_sb, AHEAD)
            act.sem_inc(yc_done, AHEAD)

            def root(g, n):
                act.wait_ge(var_ready, 4 * g + n + 1)
                act.activation(sd[:], ve[:], ACT.Sqrt).then_inc(sd_ready, 1)

            def front(g, tile, end):
                tile(0, 0)
                root(g, 0)
                tile(0, 1)
                tile(0, 2)
                act.wait_ge(diff_ready, g + 1)
                act.activation(lg[:, 2], lg[:, 1], ACT.Exp).then_inc(exp_ready, 1)

                def row(v):
                    for i in range(IMG):
                        n = IMG * (NV * g + v) + i
                        for h in range(2):
                            act.wait_ge(conv0_done, 2 * n + h + 1)
                            if h == 0:
                                act.wait_ge(sum0_done, n - 1 + AHEAD)
                            act.activation(ex0[:, i % 2, h, :], PP[2 * (i % 2) + h][:, 0:ROWN], ACT.Relu,
                                           bias=bexp[:, h:h + 1]).then_inc(relu_done, 1)
                        if i == 1:
                            tile(0, v + 3)
                    act.wait_ge(sum0_done, IMG * (NV * g + v + 1) + AHEAD)
                    act.wait_ge(win_out, 16 * (g + 1))
                    act.copy(yc[:, bass.ds(v * ROWN, ROWN)], P4[:, 0:ROWN]).then_inc(yc_done, 1)
                with act.Fori(0, NV) as v:
                    row(v)

                for t in range(TILES // 2):
                    tile(1, t)
                root(g, 1)
                act.wait_ge(z_ready, g + 1)
                act.activation(sm1[:, 2, :], sm1[:, 1, :], ACT.Exp, scale=-1.0).then_inc(ez_ready, 1)
                for t in range(TILES // 2, TILES):
                    tile(1, t)
                root(g, 2)
                act.wait_ge(xn2_ready, g + 1)

                def stage(t, i):
                    n = IMG * (TILES * g + t) + i
                    act.wait_ge(score_done, n - 3 + AHEAD)
                    act.copy(xs2[0:C, i, :], xn2[C * i:C * (i + 1), bass.ds(128 * t, 128)]
                             ).then_inc(staged2, 1)

                def turn(t, i):
                    n = IMG * (TILES * g + t) + i
                    act.wait_ge(turned, n + 1 + AHEAD)
                    act.wait_ge(q_done, n - 1 + AHEAD)
                    act.copy(onehot_t[:, i % 2, :], P2[:, :]).then_inc(turned_sb, 1)

                def codes_out(t):
                    act.wait_ge(q_done, IMG * (TILES * g + t + 1) + AHEAD)
                    act.copy(qx[:, bass.ds(t, 1), :].rearrange("p a c -> p (a c)"), P4[:, 0:128]).then_inc(qx_ready, 1)

                def body(t, first, last):
                    for i in range(IMG):
                        if i == 0:
                            stage(t, IMG - 1)
                        elif not last:
                            stage(t + 1, i - 1)
                        turn(t, i)
                        if i == 1:
                            tile(2, t)
                            if not first:
                                codes_out(t - 1)
                for i in range(IMG - 1):
                    stage(0, i)
                body(0, True, False)
                with act.Fori(1, TILES - 1) as t:
                    body(t, False, False)
                body(TILES - 1, False, True)
                codes_out(TILES - 1)

                root(g, 3)
                act.wait_ge(xn3_ready, g + 1)
                act.copy(xn2[:].rearrange("p (h w) -> p h w", w=W),
                         xp3[:, 0:G1 * G1].rearrange("p (h w) -> p h w", w=G1)[:, 1:H + 1, 1:W + 1]
                         ).then_inc(flat3_ready, 1)

                def cells_copy(i):
                    for b in range(3):
                        act.wait_ge(cells_t, IMG * g + i + 1)
                        if b == 0:
                            if i > 0:
                                act.wait_ge(tabled[i - 1], 16 * (g + 1))
                            else:
                                act.wait_ge(tabled[IMG - 1], 16 * g)
                        m = 512 if b < 2 else 128
                        act.copy(cells[:, 512 * b:512 * b + m], PP[2 + b][:, 0:m]).then_inc(cells_sb, 1)
                cells_copy(0)
                cells_copy(1)
                for t in range(TILES):
                    tile(3, t)
                    if t in (2, 5):
                        cells_copy(2 if t == 2 else 3)

            def tile(g, i, t):
                n = TILES * (IMG * g + i) + t
                act.wait_ge(samp_turned, n + 1 + AHEAD)
                act.wait_ge(conv3_done, n + AHEAD)
                act.copy(samp_t[:, 0:2, :], PT[:, 0:256].rearrange("p (r n) -> p r n", r=2)).then_inc(samp_sb, 1)
                act.copy(samp_t[0:C, 2, :], PT[0:C, 256:384]).then_inc(samp_sb, 1)

            def end(g, i):
                pass

            schedule(act, front, tile, end)

        @block.vector
        def _(dve):
            def norm(g, n, src, dst):
                for h in range(2):
                    dve.bn_stats(stats[:, h, :], src[:, h * 512:(h + 1) * 512])
                dve.drain()
                dve.bn_aggr(mv[:], stats[:])
                dve.drain()
                dve.tensor_scalar(ve[:], mv[:, 1:2], EPS, None, ALU.add).then_inc(var_ready, 1)
                dve.wait_ge(sd_ready, 4 * g + n + 1)
                dve.reciprocal(nr[:, 0:1], sd[:])
                dve.drain()
                dve.tensor_tensor(nr[:, 1:2], ve[:], nr[:, 0:1], ALU.mult)
                dve.drain()
                dve.tensor_scalar(nr[:, 2:3], nr[:, 1:2], sd[:], 0.5, ALU.add, ALU.mult)
                dve.drain()
                dve.reciprocal(nr[:, 3:4], nr[:, 2:3])
                dve.drain()
                return dve.tensor_scalar(dst, src if len(dst.shape) == 2 else src.rearrange("p (h w) -> p h w", w=W),
                                         mv[:, 0:1], nr[:, 3:4], ALU.subtract, ALU.mult)

            dve.sem_inc(onehot_ready, AHEAD)
            dve.sem_inc(fin_ready, AHEAD)
            for t in (wgrid[:], xp0[:], xp1[:], xp3[:], bd1[:], xs2[:], cb2[C:2 * C, :], cb2[2 * C:, :]):
                dve.memset(t, 0.0)
            dve.drain()
            dve.memset(xs2[C:C + 1, :, :], 1.0)
            dve.memset(negone[:], -1.0)
            dve.drain()
            dve.sem_inc(zeroed, 1)
            dve.wait_ge(loaded, LOADS)
            dve.tensor_copy(iota[:], iota_f)
            dve.tensor_copy(ident_b[:], ident[:])
            for k in range(PARTS):
                dve.tensor_copy(codes_b[:, k, :], codes[:] if k == 0 else codes_rest)
                dve.drain()
                if k < PARTS - 1:
                    dve.tensor_tensor(codes_rest, codes[:] if k == 0 else codes_rest, codes_b[:, k, :], ALU.subtract)
                    dve.drain()
            dve.tensor_tensor(cbsq, cb2[0:C, :], cb2[0:C, :], ALU.mult).then_inc(sq_ready, 1)
            dve.wait_ge(norms_ready, 1)
            dve.tensor_copy(cb2[C:C + 1, :], P0[C:C + 1, :])
            dve.tensor_scalar(cb2[0:C, :], cb2[0:C, :], 2.0, None, ALU.mult)

            def front(g, tile, end):
                tile(0, 0)
                dve.wait_ge(x_loaded, 16 * (g + 1))
                grid0 = xp0[:].rearrange("p (h w) -> p h w", w=G0)
                norm(g, 0, xres[:], grid0[:, 1:H + 1, 1:W + 1])
                dve.drain()
                for v in range(NV):
                    a = grid0[:, PS * v:PS * v + WIN, :]
                    dve.tensor_copy(win[:, NV * v:NV * (v + 1), 0:WIN * WIN].rearrange("p n (r q) -> p n r q", q=WIN),
                                    bass.AP(a.tensor, a.offset, [a.ap[0], [PS, NV], [G0, WIN], [1, WIN]]))
                a = xp0[:]
                dve.tensor_reduce(rowsum[:], bass.AP(a.tensor, a.offset, [a.ap[0], [G0, G0], [PS, NV], [1, WIN]]),
                                  AX.X, ALU.add)
                dve.drain()
                a = rowsum[:]
                dve.tensor_reduce(win[:, :, WIN * WIN].rearrange("p (v h) -> p v h", h=NV),
                                  bass.AP(a.tensor, a.offset, [a.ap[0], [PS * NV, NV], [1, NV], [NV, WIN]]),
                                  AX.X, ALU.add)
                dve.drain()
                dve.tensor_scalar(win[:, :, WIN * WIN], win[:, :, WIN * WIN], 1.0 / (WIN * WIN), None, ALU.mult
                                  ).then_inc(win_ready, 1)
                tile(0, 1)
                tile(0, 2)
                dve.wait_ge(logit_ready, g + 1)
                dve.tensor_tensor(lg[:, 0], P0[0:PATCHES, 0:IMG * E0].rearrange("p (i e) -> p i e", i=IMG),
                                  bg[:], ALU.add)
                dve.drain()
                dve.tensor_reduce(mx[:, 0], lg[:, 0], AX.X, ALU.max)
                dve.drain()

                def per_image(t):
                    return t.unsqueeze(2).broadcast_to([PATCHES, IMG, E0])
                dve.tensor_tensor(lg[:, 1], lg[:, 0], per_image(mx[:, 0]), ALU.subtract).then_inc(diff_ready, 1)
                dve.tensor_tensor(lg[:, 3], lg[:, 0], per_image(mx[:, 0]), ALU.is_equal)
                dve.drain()
                dve.tensor_tensor(lg[:, 3], lg[:, 3], rank[:], ALU.mult)
                dve.drain()
                dve.tensor_reduce(mx[:, 1], lg[:, 3], AX.X, ALU.max)
                dve.drain()
                dve.tensor_tensor(lg[:, 4], lg[:, 3], per_image(mx[:, 1]), ALU.is_equal)
                dve.wait_ge(exp_ready, g + 1)
                dve.tensor_reduce(mx[:, 2], lg[:, 2], AX.X, ALU.add)
                dve.drain()
                dve.reciprocal(mx[:, 1], mx[:, 2])
                dve.drain()
                dve.tensor_tensor(lg[:, 5], lg[:, 4], per_image(mx[:, 1]), ALU.mult).then_inc(route_ready, 1)
                dve.wait_ge(route_t, g + 1)
                dve.tensor_copy(rt_t[:], P0[0:IMG * E0, 64:64 + PATCHES]).then_inc(route_t_sb, 1)
                dve.wait_ge(route_b, g + 1)
                dve.tensor_copy(rtb[:], P1[:, 0:2 * IMG * PATCHES].rearrange("p (k n) -> p k n", n=PATCHES)
                                ).then_inc(route_ready, 1)
                dve.drain()
                with dve.Fori(0, NV) as v:
                    tile(0, v + 3, "samples")
                    for i in range(IMG):
                        n = IMG * (NV * g + v) + i
                        dve.wait_ge(relu_done, 2 * (n + 1) + AHEAD)
                        e = ex0[:, i % 2].rearrange("p h (n s) -> p h n s", s=PS * PS)
                        r = rtb[:, 2 * i:2 * i + 2, bass.ds(NV * v, NV)].unsqueeze(3)
                        dve.tensor_tensor(e, e, r.broadcast_to([128, 2, NV, PS * PS]), ALU.mult
                                          ).then_inc(gated, 1)
                    tile(0, v + 3, "sum")
                end(0)
                for t in range(TILES // 2):
                    tile(1, t)
                dve.wait_ge(y_in, 16 * (g + 1))
                for v in range(H // PS):
                    x = xres[:, PS * W * v:PS * W * (v + 1)].rearrange("p (r h q) -> p r h q", r=PS, q=PS)
                    y = yb[:, ROWN * v:ROWN * v + PS * PS * (W // PS)].rearrange("p (h r q) -> p r h q", r=PS, q=PS)
                    dve.tensor_tensor(x, x, y, ALU.add)
                dve.drain()

                grid1 = xp1[:].rearrange("p (h w) -> p h w", w=G1)[:, 1:H + 1, 1:W + 1]
                norm(g, 1, xres[:], grid1)
                dve.drain()
                dve.tensor_reduce(sm1[:, 0, 0:1], grid1, AX.XY, ALU.add)
                dve.drain()
                dve.tensor_scalar(sm1[:, 3, :], wroute[:], sm1[:, 0, 0:1], 1.0 / PIX, ALU.mult, ALU.mult
                                  ).then_inc(pooled, 1)
                dve.wait_ge(rlog_ready, g + 1)
                dve.tensor_tensor(sm1[:, 1, :], P0[:, 0:E1], broute[:], ALU.add).then_inc(z_ready, 1)
                dve.wait_ge(ez_ready, g + 1)
                dve.tensor_scalar(sm1[:, 2, :], sm1[:, 2, :], 1.0, None, ALU.add)
                dve.drain()
                dve.reciprocal(sm1[:, 0, :], sm1[:, 2, :])
                dve.drain()
                dve.tensor_scalar(mix[:], wmix[:, 0, :], sm1[:, 0, 0:1], None, ALU.mult)
                for e in range(1, E1):
                    dve.drain()
                    dve.scalar_tensor_tensor(out=mix[:], in0=wmix[:, e, :], scalar=sm1[:, 0, e:e + 1], in1=mix[:],
                                             op0=ALU.mult, op1=ALU.add)
                dve.drain()
                for i in range(IMG):
                    r = slice(C * i, C * (i + 1))
                    dve.tensor_copy(bd1[r, :, r], mix[r, :].rearrange("p (k o) -> p k o", o=C)).then_inc(bd_ready, 1)
                for t in range(TILES // 2, TILES):
                    tile(1, t)
                for h in range(2):
                    dve.wait_ge(conv1_done, 2 * g + h + 1)
                    x = xres[:, 512 * h:512 * (h + 1)]
                    dve.tensor_tensor(x, x, PP[1 + h][:, :], ALU.add).then_inc(x2_ready, 1)
                end(1)
                dve.drain()
                dve.wait_ge(off_done, g)
                norm(g, 2, xres[:], xn2[:]).then_inc(xn2_ready, 1)

                def unit(t, i):
                    n = IMG * (TILES * g + t) + i
                    dve.wait_ge(score_done, n + 1 + AHEAD)
                    dve.sem_inc(dve_passed, 1)
                    dve.max(top[:, i % 2, :], SCORES[i][:, :])
                    dve.drain()
                    dve.max_index(code[:, i % 2, :], top[:, i % 2, :], SCORES[i][:, :])
                    dve.drain()
                    dve.wait_ge(turned, n - 1 + AHEAD)
                    dve.tensor_scalar(onehot[:, i % 2, :], iota[:], code[:, i % 2, 0:1], None, ALU.is_equal
                                      ).then_inc(onehot_ready, 1)
                def units(t):
                    tile(2, t, "samples")
                    for i in range(IMG):
                        unit(t, i)
                    tile(2, t, "sum")
                units(0)
                with dve.Fori(1, TILES) as t:
                    units(t)
                end(2)
                for h in range(2):
                    c = slice(512 * h, 512 * (h + 1))
                    dve.wait_ge(qx_turned, 2 * g + h + 1)
                    dve.tensor_tensor(q2[:, c], PP[h][:, :], xn2[:, c], ALU.subtract)
                dve.tensor_copy(xlast[P - C:P, :], xfin[P - C:P, :]) if not isinstance(g, int) else None
                dve.drain()
                dve.tensor_tensor(q2[:], q2[:], xn2[:], ALU.add)
                dve.drain()
                dve.tensor_tensor(xfin[:], xres[:], q2[:], ALU.add).then_inc(x3_ready, 1)
                dve.drain()
                dve.wait_ge(xs3_loaded[1], 16 * CORN * IMG // 2 * g)
                norm(g, 3, xfin[:], xp3[:, 0:G1 * G1].rearrange("p (h w) -> p h w", w=G1)[:, 1:H + 1, 1:W + 1]
                     ).then_inc(xn3_ready, 1)
                dve.wait_ge(off_done, g + 1)
                ht = TILES // 2
                for h in range(2):
                    for a in range(2):
                        src = PP[h][:, 0:ht * IMG * 2 * TAPS].rearrange(
                            "p (t i k a) -> p a i t k", t=ht, i=IMG, a=2)[:, a]
                        dst = pos[:, a].rearrange("p i (t k) -> p i t k", k=TAPS)[:, :, ht * h:ht * (h + 1), :]
                        b = bgrid[:].rearrange("p (k a) -> p a k", a=2)[:, a].unsqueeze(1).unsqueeze(1)
                        dve.tensor_tensor(dst, src, b.broadcast_to([128, IMG, ht, TAPS]), ALU.add)
                dve.drain()
                for a in range(2):
                    dve.tensor_tensor(pos[:, a], pos[:, a],
                                      grid[:, a:a + 1, :].broadcast_to([128, IMG, TILES * TAPS]), ALU.add)
                dve.drain()
                p = pos[:].rearrange("p a i n -> p (a i n)")
                f = cell[:].rearrange("p a n -> p (a n)")
                o = over[:].rearrange("p a n -> p (a n)")
                dve.tensor_scalar(p, p, 1.0, 0.5, ALU.add, ALU.mult)
                dve.drain()
                dve.tensor_scalar(p, p, float(W - 1), -1.0, ALU.mult, ALU.max)
                dve.drain()
                dve.tensor_scalar(p, p, float(W), None, ALU.min)
                dve.drain()
                dve.tensor_copy(cell_i[:], p)
                dve.drain()
                dve.tensor_copy(f, cell_i[:])
                dve.drain()
                dve.tensor_tensor(o, f, p, ALU.is_gt)
                dve.drain()
                dve.tensor_tensor(f, f, o, ALU.subtract)
                dve.drain()
                dve.tensor_scalar(f, f, float(W - 1), None, ALU.min)
                dve.drain()
                dve.tensor_tensor(p, p, f, ALU.subtract)
                dve.scalar_tensor_tensor(out=idx[:].rearrange("p i t k -> p (i t k)"), in0=cell[:, 1],
                                         scalar=float(G1), in1=cell[:, 0], op0=ALU.mult, op1=ALU.add)
                dve.drain()
                dve.tensor_scalar(o, p, -1.0, 1.0, ALU.mult, ALU.add)
                dve.drain()
                far = pos[:].rearrange("p a i n -> p a (i n)")
                for q in range(CORN):
                    wy = (far if q // 2 else over)[:, 1]
                    wx = (far if q % 2 else over)[:, 0]
                    dve.tensor_tensor(wq[:].rearrange("p i t (k q) -> p (i t k) q", q=CORN)[:, :, q], wx, wy, ALU.mult)
                dve.drain()
                if isinstance(g, int):
                    for t in range(TILES):
                        stage_slot(0, t)
                for t in range(TILES):
                    tile(3, t)
                end(3)

            def stage_slot(i, t):
                dve.tensor_copy(w_slot[:, bass.ds(t, 1), :], wq[:, i, bass.ds(t, 1), :])
                dve.tensor_scalar(idx_slot[:, bass.ds(t, 1), :], idx[:, i, bass.ds(t, 1), :], float(G1 + 1), None,
                                  ALU.add).then_inc(granted, 1)

            def residual(g, i, t):
                dve.wait_ge(conv3_done, TILES * (IMG * g + i) + t + 1 + AHEAD)
                src = xlast if i == IMG - 1 and not isinstance(g, int) else xfin
                r = slice(C * i, C * (i + 1))
                dve.tensor_tensor(fin[r, bass.ds(128 * t, 128)], src[r, bass.ds(128 * t, 128)], PO[r, 0:128],
                                  ALU.add).then_inc(fin_ready, 1)

            def tile(g, i, t, part="both"):
                if part != "sum":
                    n = TILES * (IMG * g + i) + t
                    dve.wait_ge(tile_ready, n + 1)
                    s = ring[:, bass.ds(t, 1), :].rearrange("p a (n c) -> p (a n) c", c=C)
                    w = w_slot[:, bass.ds(t, 1), :].rearrange("p a n -> p (a n)").unsqueeze(2)
                    dve.tensor_tensor(s, s, w.broadcast_to([128, TAPS * CORN, C]), ALU.mult)
                    dve.drain()
                    s = ring[:, bass.ds(t, 1), :].rearrange("p a (k y n) -> p (a k) y n", k=TAPS, y=2)
                    dve.tensor_tensor(pair[:].rearrange("p k x c -> p k (x c)"), s[:, :, 0], s[:, :, 1], ALU.add)
                    dve.drain()
                    if not (isinstance(g, int) and i == IMG - 1):
                        stage_slot((i + 1) % IMG, t)
                    dve.wait_ge(samp_turned, n + AHEAD)
                    dve.tensor_tensor(samp[:].rearrange("p (k c) -> p k c", c=C), pair[:, :, 0], pair[:, :, 1],
                                      ALU.add).then_inc(samp_ready, 1)
                if part != "samples":
                    if isinstance(t, int) and t == 0:
                        dve.wait_ge(stored, 16 * (IMG * (g - 1) + i + 1) + STORED_AHEAD)
                        dve.sem_inc(dve_passed, 1)
                    else:
                        residual(g, i, t - 1)

            def end(g, i):
                residual(g, i, TILES - 1)

            schedule(dve, front, tile, end)

        @block.tensor
        def _(pe):
            pe.sem_inc(sum0_done, AHEAD)
            pe.sem_inc(score_done, AHEAD)
            pe.sem_inc(q_done, AHEAD)
            pe.sem_inc(turned, AHEAD)
            pe.sem_inc(samp_turned, AHEAD)
            pe.sem_inc(conv3_done, AHEAD)
            pe.wait_ge(sq_ready, 1)
            pe.matmul(P0[C:C + 1, :], negone[:], cbsq, start=True, stop=True).then_inc(norms_ready, 1)

            def front(g, tile, end):
                for t in range(3):
                    tile(0, t)
                pe.wait_ge(xs0_loaded, 16 * 3 * IMG * (g + 1))
                pe.sem_inc(pe_passed, 1)
                for i in range(IMG):
                    m = pe.matmul(P0[0:PATCHES, E0 * i:E0 * (i + 1)], xs0[2 * C:3 * C, i, :, CUT - 1],
                                  wg[2 * C:3 * C, :], start=True, stop=True)
                m.then_inc(logit_ready, 1)
                pe.wait_ge(route_ready, 2 * g + 1)
                pe.sem_inc(pe_passed, 1)
                pe.transpose(P0[0:IMG * E0, 64:64 + PATCHES], lg[:, 5].rearrange("p i e -> p (i e)"),
                             ident[0:PATCHES, 0:PATCHES]).then_inc(route_t, 1)
                pe.wait_ge(route_t_sb, g + 1)
                pe.wait_ge(cells_sb, 3 * IMG * g)
                for k in range(2 * IMG):
                    m = pe.matmul(P1[:, PATCHES * k:PATCHES * (k + 1)], pick[:, k, :], rt_t[:], start=True, stop=True)
                m.then_inc(route_b, 1)
                pe.wait_ge(route_ready, 2 * g + 2)
                pe.sem_inc(pe_passed, 1)

                def conv(v, i):
                    n = IMG * (NV * g + v) + i
                    pe.wait_ge(relu_done, 2 * (n - 1) + AHEAD)
                    for h in range(2):
                        for dx in range(3):
                            a = xs0[:, i, bass.ds(NV * v, NV), dx:CUT - 1]
                            a = bass.AP(a.tensor, a.offset, [a.ap[0], [CUT, NV], [WIN, PS], [1, PS]])
                            m = pe.matmul(PP[2 * (i % 2) + h][:, 0:ROWN], w0[:, dx, h, :], a,
                                          start=(dx == 0), stop=(dx == 2))
                        m.then_inc(conv0_done, 1)

                def add_up(v, i):
                    n = IMG * (NV * g + v) + i
                    pe.wait_ge(gated, n + 1)
                    if i == 0:
                        pe.wait_ge(yc_done, NV * g + v + AHEAD)
                    for h in range(2):
                        m = pe.matmul(P4[C * i:C * (i + 1), 0:ROWN], sume[:], ex0[:, i % 2, h, :],
                                      start=(h == 0), stop=(h == 1))
                    m.then_inc(sum0_done, 1)
                with pe.Fori(0, NV) as v:
                    for i in range(IMG):
                        conv(v, i)
                        if i:
                            add_up(v, i - 1)
                        if i == 1:
                            tile(0, v + 3)
                    add_up(v, IMG - 1)
                end(0)
                for t in range(TILES // 2):
                    tile(1, t)

                pe.wait_ge(pooled, g + 1)
                pe.matmul(P0[:, 0:E1], same[:], sm1[:, 3, :], start=True, stop=True).then_inc(rlog_ready, 1)
                pe.wait_ge(bd_ready, IMG * (g + 1))
                grid1 = xp1[:].rearrange("p (h w) -> p h w", w=G1)
                for h in range(2):
                    for k in range(TAPS):
                        y = H // 2 * h + k // 3
                        m = pe.matmul(PP[1 + h][:, :], bd1[:, k, :], grid1[:, y:y + H // 2, k % 3:k % 3 + W],
                                      start=(k == 0), stop=(k == TAPS - 1))
                        if k == TAPS // 2:
                            tile(1, TILES // 2 + 2 * h)
                    m.then_inc(conv1_done, 1)
                    tile(1, TILES // 2 + 2 * h + 1)
                end(1)
                pe.wait_ge(x2_ready, 2 * (g + 1))

                def scores(t, i):
                    n = IMG * (TILES * g + t) + i
                    pe.wait_ge(staged2, n + 1)
                    pe.wait_ge(onehot_ready, n - 3 + AHEAD)
                    pe.matmul(SCORES[i][:, :], xs2[:, i, :], cb2[:], start=True, stop=True).then_inc(score_done, 1)

                def turn(t, i):
                    n = IMG * (TILES * g + t) + i
                    pe.wait_ge(onehot_ready, n + 1 + AHEAD)
                    pe.wait_ge(turned_sb, n + AHEAD)
                    for c in range(CCH):
                        m = pe.matmul(P2[:, 128 * c:128 * (c + 1)], onehot[:, i % 2, 128 * c:128 * (c + 1)],
                                      ident_b[:], start=True, stop=True)
                    m.then_inc(turned, 1)

                def pick_code(t, i):
                    n = IMG * (TILES * g + t) + i
                    pe.wait_ge(turned_sb, n + 1 + AHEAD)
                    if i == 0:
                        pe.wait_ge(qx_ready, TILES * g + t)
                    for c in range(CCH):
                        for k in range(PARTS):
                            m = pe.matmul(P4[:, C * i:C * (i + 1)], onehot_t[:, i % 2, 128 * c:128 * (c + 1)],
                                          codes_b[:, k, C * c:C * (c + 1)],
                                          start=(c == 0 and k == 0), stop=(c == CCH - 1 and k == PARTS - 1))
                    m.then_inc(q_done, 1)

                def body(t, first):
                    for i in range(IMG):
                        scores(t, i)
                        if i >= 2 or not first:
                            turn(t if i >= 2 else t - 1, (i - 2) % IMG)
                        if i >= 3 or not first:
                            pick_code(t if i >= 3 else t - 1, (i - 3) % IMG)
                        if i == 1:
                            tile(2, t)
                body(0, True)
                with pe.Fori(1, TILES) as t:
                    body(t, False)
                turn(TILES - 1, IMG - 2)
                pick_code(TILES - 1, IMG - 3)
                turn(TILES - 1, IMG - 1)
                pick_code(TILES - 1, IMG - 2)
                pick_code(TILES - 1, IMG - 1)
                pe.wait_ge(qx_ready, TILES * (g + 1))
                for t in range(TILES):
                    m = pe.transpose(PP[t // 4][:, 128 * (t % 4):128 * (t % 4 + 1)], qx[:, t, :], ident[:])
                    if t % 4 == 3:
                        m.then_inc(qx_turned, 1)
                end(2)

                pe.wait_ge(flat3_ready, g + 1)
                ht = TILES // 2
                for t in range(TILES):
                    n = IMG * 2 * TAPS
                    m = pe.matmul(PP[t // ht][:, n * (t % ht):n * (t % ht + 1)],
                                  xn2[:, 128 * t:128 * (t + 1)], wgrid[:], start=True, stop=True)
                m.then_inc(off_done, 1)

                def table_t(i):
                    pe.wait_ge(xs3_loaded[i % 2], 16 * CORN * (IMG // 2 * g + i // 2 + 1))
                    pe.wait_ge(cells_sb, 3 * (IMG * g + i))
                    for c in range(TROWS // 128):
                        m = pe.transpose(PP[2 + c // 4][:, 128 * (c % 4):128 * (c % 4 + 1)],
                                         xs3[:, i % 2, 128 * c:128 * (c + 1)], ident[:])
                    m.then_inc(cells_t, 1)
                table_t(0)
                table_t(1)
                for t in range(TILES):
                    tile(3, t)
                    if t in (2, 5):
                        table_t(2 if t == 2 else 3)
                end(3)

            def convolve(g, i, t):
                n = TILES * (IMG * g + i) + t
                pe.wait_ge(samp_sb, 2 * (n + 1))
                pe.wait_ge(fin_ready, n + AHEAD)
                for r in range(3):
                    k = min(128, TC - 128 * r)
                    m = pe.matmul(PO[C * i:C * (i + 1), 0:128], wc[0:k, r, :], samp_t[0:k, r, :],
                                  start=(r == 0), stop=(r == 2))
                m.then_inc(conv3_done, 1)

            def tile(g, i, t):
                if not (isinstance(t, int) and t == 0):
                    convolve(g, i, t - 1)
                pe.wait_ge(samp_ready, TILES * (IMG * g + i) + t + 1)
                for r in range(3):
                    k = min(128, TC - 128 * r)
                    m = pe.transpose(PT[0:k, 128 * r:128 * (r + 1)], samp[:, 128 * r:128 * r + k], ident[:])
                m.then_inc(samp_turned, 1)

            def end(g, i):
                convolve(g, i, TILES - 1)

            schedule(pe, front, tile, end)


LOADS = 16 * (10 + IMG + 2 * IMG + 5 + 3)


def constants():
    f = np.float32
    pick = np.zeros((IMG * E0, 2 * IMG, 128), f)
    for i in range(IMG):
        for e in range(E0):
            pick[i * E0 + e, 2 * i + e // HALF, (e % HALF) * C:(e % HALF + 1) * C] = 1
    grid = np.zeros((128, 2, TILES, TAPS), f)
    base = np.linspace(-1.0, 1.0, W, dtype=f)
    koff = np.linspace(-2 / (W - 1), 2 / (W - 1), 3, dtype=f)
    for t in range(TILES):
        for p in range(128):
            y, x = divmod(128 * t + p, W)
            for k in range(TAPS):
                grid[p, 0, t, k] = base[x] + koff[k % 3]
                grid[p, 1, t, k] = base[y] + koff[k // 3]
    return {
        "ident": np.eye(128, dtype=f),
        "pick_expert": pick,
        "sum_experts": np.tile(np.eye(C, dtype=f), (HALF, 1)),
        "same_image": np.kron(np.eye(IMG, dtype=f), np.ones((C, C), f)),
        "code_iota": np.tile(np.arange(CODES, dtype=f), (128, 1)),
        "first_rank": np.tile(np.arange(E0, 0, -1, dtype=f), (PATCHES, IMG, 1)),
        "grid": grid.reshape(128, 2, TILES * TAPS),
    }


def kernel(**inputs):
    import concourse.bacc as bacc
    from concourse.bass_utils import run_bass_kernel_spmd

    a = {k: np.asarray(v) for k, v in inputs.items()}
    arrays = {
        "x": a["x"].reshape(B * C, PIX),
        "Wg": a["L0_conv_Wg"],
        "bg": np.broadcast_to(a["L0_conv_bg"], (IMG, E0)),
        "Wexp": a["L0_conv_Wexp"].transpose(3, 2, 4, 0, 1).reshape(3 * C, 3, 2, HALF * C),
        "bexp": a["L0_conv_bexp"].reshape(2, HALF * C).T,
        "w_route": a["L1_conv_w_route"].T,
        "b_route": a["L1_conv_b_route"],
        "w_mix": a["L1_conv_w_experts"].transpose(2, 0, 3, 4, 1).reshape(C, E1, TC),
        "codebook": a["L2_conv_codebook"],
        "codebook_t": a["L2_conv_codebook"].T,
        "w_grid": a["L3_conv_w_grid"].T,
        "b_grid": a["L3_conv_b_grid"],
        "w_conv": a["L3_conv_w_conv"].transpose(2, 3, 1, 0).reshape(TC, C),
    }
    arrays.update(constants())
    arrays = {f"in_{k}": np.ascontiguousarray(v) for k, v in arrays.items()}
    nc = bacc.Bacc("TRN2", target_bir_lowering=False, num_devices=1)
    aps = {k: nc.dram_tensor(f"in_{k}", arrays[f"in_{k}"].shape, mybir.dt.from_np(arrays[f"in_{k}"].dtype),
                             kind="ExternalInput").ap() for k in INPUTS}
    aps["out"] = nc.dram_tensor("out", (B * C, PIX), F32, kind="ExternalOutput").ap()
    build(nc, aps, aps["out"])
    r = run_bass_kernel_spmd(nc, [arrays], core_ids=[0])
    return r.results[0]["out"].reshape(B, C, H, W)
```

```python
from contextlib import ExitStack

import numpy as np

import concourse.bass as bass
from concourse import mybir

ALU = mybir.AluOpType
ACT = mybir.ActivationFunctionType
AX = mybir.AxisListType
F32 = mybir.dt.float32
U32 = mybir.dt.uint32
BF16 = mybir.dt.bfloat16
F16 = mybir.dt.float16

B, C, H, W = 32, 32, 32, 32
PIX = H * W
IMG = 4
GROUPS = B // IMG
P = IMG * C
PS = 8
NV = H // PS + 1
PATCHES = NV * NV
WIN = PS + 2
G0 = NV * PS + 2
WROW = WIN * WIN
CUT = PS * WIN
E0 = 8
HALF = 4
ROWN = NV * PS * PS
E1 = 4
G1 = W + 2
TAPS = 9
CODES = 512
CCH = CODES // 128
TILES = PIX // 128
CORN = 4
CHUNKS = -(-(W + 1) * G1 // 128)
TROWS = CHUNKS * 128
XP3 = TROWS + G1 + 2
ROW = TAPS * CORN * C
TC = TAPS * C
EPS = 1e-5
AHEAD = 3
STORED_AHEAD = 16 * (IMG + 1)
GATHERED = 4
SEEN_AT = 5
BUSY = range(4, 7)
WHOLE = float(3 << 22)
PARTS = 3

INPUTS = ["x", "Wg", "bg", "Wexp", "bexp", "w_route", "b_route", "w_mix", "codebook", "codebook_t",
          "w_grid", "b_grid", "w_conv", "ident", "pick_expert", "sum_experts", "same_image",
          "code_iota", "first_rank", "grid"]


def build(nc, A):
    ctx = ExitStack()
    with ctx:
        def sb(name, shape, dt=F32):
            return ctx.enter_context(nc.sbuf_tensor(name, shape, dt))

        def bank(name):
            return ctx.enter_context(nc.psum_tensor(name, [128, 512], F32))

        def sem(name):
            return ctx.enter_context(nc.semaphore(name))

        ident = sb("ident_sb", [128, 128])
        pick = sb("pick_sb", [IMG * E0, 2 * IMG, 128])
        sume = sb("sume_sb", [128, C])
        same = sb("same_sb", [128, 128])
        iota = sb("iota_sb", [128, CODES], F16)
        rank = sb("rank_sb", [PATCHES, IMG, E0])
        grid = sb("grid_sb", [128, 2, TILES * TAPS])
        w0 = sb("w0", [3 * C, 3, 2, 128])
        bexp = sb("bexp_sb", [128, 2])
        wg = sb("wg_sb", [128, IMG * E0])
        bg = sb("bg_sb", [PATCHES, IMG, E0])
        wmix = sb("wmix", [128, E1, TC])
        wroute = sb("wroute", [128, E1])
        broute = sb("broute", [128, E1])
        cb2 = sb("cb2", [128, CODES])
        negone = sb("negone", [C, 1])
        codes = sb("codes", [128, CCH * C])
        codes_b = sb("codes_b", [128, PARTS, CCH * C], BF16)
        wgrid = sb("wgrid", [128, IMG * 2 * TAPS])
        bgrid = sb("bgrid", [128, 2 * TAPS])
        wc = sb("wc", [128, 3, C])
        xres = sb("xres", [128, PIX])
        xfin = sb("xfin", [128, PIX])
        xlast = sb("xlast", [128, PIX])
        stats = sb("stats", [128, 2, 6])
        mv = sb("mv", [128, 2])
        ve = sb("ve", [128, 1])
        sd = sb("sd", [128, 1])
        nr = sb("nr", [128, 4])
        xp0 = sb("xp0", [128, G0 * G0])
        arena = sb("arena", [128, IMG * PATCHES * CUT])
        xs0 = arena[0:3 * C, :].rearrange("p (i n s) -> p i n s", i=IMG, s=CUT)
        cells = arena[:, 0:IMG * TROWS].rearrange("p (i n q c) -> p i n q c", i=IMG, q=CORN, c=C)
        cbsq = xlast[0:C, 0:CODES]
        iota_f = xfin[:, 0:CODES]
        codes_rest = xfin[:, CODES:CODES + CCH * C]
        qx = arena[:, 0:PIX].rearrange("p (t c) -> p t c", c=128)
        wsum = sb("wsum", [128, PATCHES])
        feat = sb("feat", [PATCHES, 128])
        feat_t = sb("feat_t", [128, PATCHES])
        rowsum = sb("rowsum", [128, G0, NV])
        lg = sb("lg", [PATCHES, 6, IMG, E0])
        mx = sb("mx", [PATCHES, 3, IMG])
        rt_t = sb("rt_t", [IMG * E0, PATCHES])
        rtb = sb("rtb", [128, 2 * IMG, PATCHES])
        ex0 = sb("ex0", [128, IMG, 2, ROWN])
        blocks = sb("blocks", [128, 2 * NV * ROWN])
        win = blocks[:, 0:PATCHES * WROW].rearrange("p (n s) -> p n s", s=WROW)
        yc = blocks[:, 0:NV * ROWN]
        yb = blocks[:, NV * ROWN:2 * NV * ROWN]
        xp1 = sb("xp1", [128, G1 * G1])
        sm1 = sb("sm1", [128, 4, E1])
        mix = sb("mix", [128, TC])
        bd1 = sb("bd1", [128, TAPS, 128])
        xn2 = sb("xn2", [128, PIX])
        xs2 = sb("xs2", [128, IMG, 128])
        onehot = sb("onehot", [128, 2, CODES], BF16)
        onehot_t = sb("onehot_t", [128, 2, CODES], BF16)
        ident_b = sb("ident_b", [128, 128], BF16)
        top = sb("top", [128, 2, 8])
        code = sb("code", [128, 2, 8], U32)
        q2 = sb("q2", [128, PIX])
        xp3 = sb("xp3", [128, XP3])
        pos = sb("pos", [128, 2, IMG, TILES * TAPS])
        cell = sb("cell", [128, 2, IMG, TILES * TAPS])
        over = sb("over", [128, 2, IMG, TILES * TAPS])
        idx = sb("idx_sb", [128, IMG, TILES, TAPS], U32)
        wlast = sb("wlast", [128, TILES, TAPS * CORN])
        wq = sb("wq", [128, IMG, TILES, TAPS * CORN])
        ring = sb("ring", [128, TILES, ROW])
        pair = sb("pair", [128, TAPS, 2, C])
        samp = sb("samp", [128, TC])
        samp_t = sb("samp_t", [128, 3, 128])
        fin = sb("fin", [128, PIX])

        P0, P1, P2, P3, P4, P5, PT, PO = [bank(f"bank{n}") for n in range(8)]
        PP = [P0, P1, P2, P3, P4]
        SCORES = [P0, P1, P3, P5]
        CELLS = [P2, P3, P4]

        win_dram = nc.dram_tensor("windows", [IMG, C * PATCHES, WROW], F32).ap()
        sum_dram = nc.dram_tensor("window_means", [IMG, C * PATCHES], F32).ap()
        y_dram = nc.dram_tensor("y_patches", [IMG, C * PATCHES, PS * PS], F32).ap()
        table = [nc.dram_tensor(f"cells_{i}", [TROWS, CORN * C], F32).ap() for i in range(IMG)]

        loaded = sem("loaded")
        loaded_later = sem("loaded_later")
        zeroed = sem("zeroed")
        sq_ready = sem("sq_ready")
        norms_ready = sem("norms_ready")
        x_loaded = sem("x_loaded")
        x3_ready = sem("x3_ready")
        var_ready = sem("var_ready")
        sd_ready = sem("sd_ready")
        win_ready = sem("win_ready")
        win_out = [sem(f"win_out{i}") for i in range(IMG)]
        xs0_loaded = sem("xs0_loaded")
        wsum_ready = sem("wsum_ready")
        wsum_out = sem("wsum_out")
        feat_loaded = sem("feat_loaded")
        feat_turned = sem("feat_turned")
        feat_sb = sem("feat_sb")
        logit_ready = sem("logit_ready")
        diff_ready = sem("diff_ready")
        exp_ready = sem("exp_ready")
        route_ready = sem("route_ready")
        route_t = sem("route_t")
        route_t_sb = sem("route_t_sb")
        route_b = sem("route_b")
        conv0_done = sem("conv0_done")
        relu_done = sem("relu_done")
        gated = sem("gated")
        sum0_done = sem("sum0_done")
        yc_done = sem("yc_done")
        y_out = [sem(f"y_out{i}") for i in range(IMG)]
        y_in = sem("y_in")
        pooled = sem("pooled")
        rlog_ready = sem("rlog_ready")
        z_ready = sem("z_ready")
        ez_ready = sem("ez_ready")
        bd_ready = sem("bd_ready")
        conv1_done = sem("conv1_done")
        x2_ready = sem("x2_ready")
        xn2_ready = sem("xn2_ready")
        staged2 = sem("staged2")
        score_done = sem("score_done")
        onehot_ready = sem("onehot_ready")
        turned = sem("turned")
        turned_sb = sem("turned_sb")
        q_done = sem("q_done")
        qx_ready = sem("qx_ready")
        qx_turned = sem("qx_turned")
        xn3_ready = sem("xn3_ready")
        flat3_ready = sem("flat3_ready")
        off_done = sem("off_done")
        cells_t = sem("cells_t")
        cells_sb = sem("cells_sb")
        tabled = [sem(f"tabled{i}") for i in range(IMG)]
        granted = sem("granted")
        gathered = [sem(f"gathered{t}") for t in range(GATHERED)]
        tile_ready = sem("tile_ready")
        samp_ready = sem("samp_ready")
        samp_turned = sem("samp_turned")
        samp_sb = sem("samp_sb")
        conv3_done = sem("conv3_done")
        result_sb = sem("result_sb")
        fin_ready = sem("fin_ready")
        stored = sem("stored")

        pe_passed, dve_passed = sem("pe_passed"), sem("dve_passed")
        pool_passed, sp_passed = sem("pool_passed"), sem("sp_passed")
        act_passed = sem("act_passed")

        block = ctx.enter_context(nc.Block())

        def schedule(eng, front, image_tiles):
            front(0, None)
            with eng.Fori(0, GROUPS - 1) as g:
                front(g + 1, g)
            for i in range(IMG):
                image_tiles(GROUPS - 1, i)

        @block.sync
        def _(sp):
            sp.sem_inc(stored, STORED_AHEAD)
            for dst, src in (
                (ident[:], A["ident"]), (pick[:], A["pick_expert"]), (sume[:], A["sum_experts"]),
                (same[:], A["same_image"]), (rank[:], A["first_rank"]), (grid[:], A["grid"]),
                (w0[:], A["Wexp"]), (bexp[:], A["bexp"]), (bg[:], A["bg"].partition_broadcast(PATCHES)),
            ):
                sp.dma_start(dst, src).then_inc(loaded, 16)
            sp.wait_ge(zeroed, 1)
            for i in range(IMG):
                r = slice(C * i, C * (i + 1))
                sp.dma_start(wg[r, E0 * i:E0 * (i + 1)], A["Wg"]).then_inc(loaded, 16)
            for i in range(IMG):
                r = slice(C * i, C * (i + 1))
                sp.dma_start(wgrid[r, 2 * TAPS * i:2 * TAPS * (i + 1)], A["w_grid"]).then_inc(loaded, 16)

            def store(b, i):
                if b is None:
                    return
                sp.wait_ge(fin_ready, IMG * b + i + 1)
                sp.wait_ge(stored, 16 * (IMG * b + i) + STORED_AHEAD)
                rows = A["out"].rearrange("(n p) m -> n p m", p=C)
                sp.dma_start(rows[bass.ds(IMG * b + i, 1)].rearrange("n p m -> (n p) m"),
                             fin[C * i:C * (i + 1), :]).then_inc(stored, 16)

            def front(g, b):
                sp.wait_ge(wsum_ready, g + 1)
                sp.dma_start(sum_dram.rearrange("i (c n) -> (i c) n", c=C), wsum[:]).then_inc(wsum_out, 16)
                sp.wait_ge(wsum_out, 16 * (g + 1))
                sp.dma_start(feat[:].rearrange("n (i c) -> n i c", i=IMG),
                             sum_dram.rearrange("i (n c) -> n i c", c=C)).then_inc(feat_loaded, 16)
                sp.wait_ge(win_ready, g + 1)
                sp.sem_inc(sp_passed, 1)
                sp.wait_ge(xs0_loaded, 16 * 3 * IMG * g)
                sp.sem_inc(sp_passed, 1)
                for i in range(IMG):
                    sp.dma_start(win_dram[i].rearrange("(c n) s -> c (n s)", c=C),
                                 win[C * i:C * (i + 1)].rearrange("p n s -> p (n s)")).then_inc(win_out[i], 16)
                sp.wait_ge(tabled[IMG - 1], 16 * g)
                sp.sem_inc(sp_passed, 1)
                for i in range(IMG):
                    sp.wait_ge(win_out[i], 16 * (g + 1))
                    sp.sem_inc(sp_passed, 1)
                    for dy in range(3):
                        sp.dma_start(xs0[C * dy:C * (dy + 1), i, :, :],
                                     win_dram[i].rearrange("(p c) s -> c p s", c=C)[:, :, dy * WIN:dy * WIN + CUT]
                                     ).then_inc(xs0_loaded, 16)
                most = (NV - 1) * NV
                full = most * C // PATCHES
                for part, (rows, n0, n1, c0, c1) in enumerate(
                        ((NV - 1, 0, most, 0, full), (NV, most, PATCHES, full, C))):
                    sp.wait_ge(yc_done, NV * g + rows + AHEAD)
                    sp.sem_inc(sp_passed, 1)
                    if part == 0:
                        sp.wait_ge(y_in, 16 * 2 * IMG * g)
                        sp.sem_inc(sp_passed, 1)
                    for i in range(IMG):
                        sp.dma_start(y_dram[i].rearrange("(p c) s -> c p s", c=C)[:, n0:n1],
                                     yc[C * i:C * (i + 1), PS * PS * n0:PS * PS * n1].rearrange(
                                         "c (p s) -> c p s", s=PS * PS)).then_inc(y_out[i], 16)
                    for i in range(IMG):
                        sp.wait_ge(y_out[i], 16 * (2 * g + part + 1))
                        sp.sem_inc(sp_passed, 1)
                        sp.dma_start(yb[C * i + c0:C * i + c1, :],
                                     y_dram[i].rearrange("(c n) s -> c (n s)", c=C)[c0:c1]).then_inc(y_in, 16)
                store(b, 0)
                store(b, 1)

                def write_table(i):
                    sp.wait_ge(cells_sb, CHUNKS * (g + 1))
                    sp.sem_inc(sp_passed, 1)
                    if not isinstance(g, int):
                        sp.wait_ge(samp_ready, TILES * (IMG * (g - 1) + i + 1))
                        sp.sem_inc(sp_passed, 1)
                    sp.dma_start(table[i].rearrange("(n p) c -> p n c", p=128),
                                 cells[:, i].rearrange("p n q c -> p n (q c)")).then_inc(tabled[i], 16)
                for i in range(IMG):
                    write_table(i)
                    if i == 0:
                        store(b, 2)
                store(b, 3)

            schedule(sp, front, store)
            sp.wait_ge(stored, 16 * B + STORED_AHEAD)

        @block.gpsimd
        def _(pool):
            for i in range(IMG):
                r = slice(C * i, C * (i + 1))
                pool.dma_start(wmix[r], A["w_mix"]).then_inc(loaded_later, 16)
                pool.dma_start(wroute[r], A["w_route"]).then_inc(loaded_later, 16)
            pool.dma_start(broute[:], A["b_route"].partition_broadcast(128)).then_inc(loaded_later, 16)
            pool.dma_start(cb2[0:C, :], A["codebook_t"]).then_inc(loaded_later, 16)
            pool.dma_start(codes[:].rearrange("p (k c) -> p k c", c=C),
                           A["codebook"].rearrange("(k p) c -> p k c", p=128)).then_inc(loaded_later, 16)
            pool.dma_start(iota_f, A["code_iota"]).then_inc(loaded_later, 16)
            pool.dma_start(bgrid[:], A["b_grid"].partition_broadcast(128)).then_inc(loaded_later, 16)
            for r in range(3):
                n = min(128, TC - 128 * r)
                pool.dma_start(wc[0:n, r, :], A["w_conv"][128 * r:128 * r + n, :]).then_inc(loaded_later, 16)

            def seen(n):
                pool.wait_ge(gathered[n % GATHERED],
                             16 * TAPS * (TILES * IMG // GATHERED * g + n // GATHERED + 1))
                pool.sem_inc(tile_ready, 1)

            with pool.Fori(0, GROUPS) as g:
                for i in range(IMG):
                    pool.wait_ge(tabled[i], 16 * (g + 1))
                    for t in range(TILES):
                        n = TILES * i + t
                        pool.wait_ge(granted, IMG * TILES * g + n + 1)
                        pool.sem_inc(pool_passed, 1)
                        for k in range(TAPS):
                            pool.indirect_dma_start(
                                ring[:, t, CORN * C * k:CORN * C * (k + 1)], None, table[i],
                                bass.IndirectOffsetOnAxis(ap=idx[:, i, t, k:k + 1], axis=0),
                            ).then_inc(gathered[t % GATHERED], 16)
                            if k == SEEN_AT:
                                for m in range(max(0, n - 2), n):
                                    if n == m + (2 if m + 1 in BUSY else 1):
                                        seen(m)
                seen(IMG * TILES - 1)

        @block.scalar
        def _(act):
            act.sem_inc(relu_done, AHEAD)
            act.sem_inc(turned_sb, AHEAD)
            act.sem_inc(yc_done, AHEAD)
            act.sem_inc(result_sb, AHEAD)

            def load_x(g):
                act.wait_ge(x3_ready, g)
                act.dma_start(xres[:], A["x"].rearrange("(g p) n -> g p n", p=P)[bass.ds(g, 1)]
                             .rearrange("g p n -> (g p) n")).then_inc(x_loaded, 16)

            def root(g, n):
                act.wait_ge(var_ready, 4 * g + n + 1)
                act.activation(sd[:], ve[:], ACT.Sqrt).then_inc(sd_ready, 1)

            def front(g, b):
                load_x(g)
                clear(b, 0)
                copy_samples(b, 0, 0)
                root(g, 0)
                copy_result(b, 0, 0)
                act.wait_ge(diff_ready, g + 1)
                act.activation(lg[:, 2], lg[:, 1], ACT.Exp).then_inc(exp_ready, 1)
                tiles(b, 0, 1, 6)

                def relu(v, i):
                    n = IMG * (NV * g + v) + i
                    for h in range(2):
                        act.wait_ge(conv0_done, 2 * n + h + 1)
                        act.activation(ex0[:, i, h, :], PP[2 * (i % 2) + h][:, 0:ROWN], ACT.Relu,
                                       bias=bexp[:, h:h + 1]).then_inc(relu_done, 1)

                def sums(v):
                    act.wait_ge(sum0_done, NV * g + v + 1 + AHEAD)
                    act.copy(yc[:, bass.ds(v * ROWN, ROWN)], P4[:, 0:ROWN]).then_inc(yc_done, 1)

                def row(v, i, t):
                    relu(v, 0)
                    relu(v, 1)
                    copy_samples(b, i, t)
                    relu(v, 2)
                    copy_samples(b, i, t + 1)
                    copy_result(b, i, t)
                    relu(v, 3)
                    copy_result(b, i, t + 1)
                row(0, 0, 6)
                for i in range(IMG):
                    act.wait_ge(win_out[i], 16 * (g + 1))
                clear(b, 1)
                with act.Fori(1, NV) as v:
                    sums(v - 1)
                    row(v, 1, 2 * v - 2)
                sums(NV - 1)
                clear(b, 2)
                tiles(b, 2, 0, 2)
                root(g, 1)
                act.wait_ge(z_ready, g + 1)
                act.activation(sm1[:, 2, :], sm1[:, 1, :], ACT.Exp, scale=-1.0).then_inc(ez_ready, 1)
                tiles(b, 2, 2, 5)
                root(g, 2)
                act.wait_ge(xn2_ready, g + 1)

                def stage(t, i):
                    n = IMG * (TILES * g + t) + i
                    act.wait_ge(score_done, n - 3 + AHEAD)
                    act.copy(xs2[0:C, i, :], xn2[C * i:C * (i + 1), bass.ds(128 * t, 128)]
                             ).then_inc(staged2, 1)

                def turn(t, i):
                    n = IMG * (TILES * g + t) + i
                    act.wait_ge(turned, n + 1 + AHEAD)
                    act.wait_ge(q_done, n - 1 + AHEAD)
                    act.copy(onehot_t[:, i % 2, :], P2[:, :]).then_inc(turned_sb, 1)

                def codes_out(t):
                    act.wait_ge(q_done, IMG * (TILES * g + t + 1) + AHEAD)
                    act.copy(qx[:, bass.ds(t, 1), :].rearrange("p a c -> p (a c)"), P4[:, 0:128]).then_inc(qx_ready, 1)

                def body(t, first, last):
                    for i in range(IMG):
                        if not last:
                            stage(t + 1, i)
                        turn(t, i)
                        if i == 0 and first:
                            tiles(b, 2, 6, 7)
                        if i == 1 and not first:
                            codes_out(t - 1)
                for i in range(IMG):
                    stage(0, i)
                tiles(b, 2, 5, 6)
                body(0, True, False)
                with act.Fori(1, TILES - 1) as t:
                    body(t, False, False)
                body(TILES - 1, False, True)
                codes_out(TILES - 1)
                tiles(b, 2, 7, 8)

                root(g, 3)
                act.wait_ge(xn3_ready, g + 1)
                act.copy(xn2[:].rearrange("p (h w) -> p h w", w=W),
                         xp3[:, 0:G1 * G1].rearrange("p (h w) -> p h w", w=G1)[:, 1:H + 1, 1:W + 1]
                         ).then_inc(flat3_ready, 1)

                for i in range(IMG):
                    act.wait_ge(tabled[i], 16 * g)
                    act.sem_inc(act_passed, 1)

                def cells_copy(first, end):
                    for k in range(first, end):
                        act.wait_ge(cells_t, CHUNKS * g + k + 1)
                        act.copy(cells[:, :, k], CELLS[k % 3][:].rearrange("p (q i c) -> p i q c", q=CORN, i=IMG)
                                 ).then_inc(cells_sb, 1)
                cells_copy(0, 3)
                clear(b, 3)
                copy_samples(b, 3, 0)
                cells_copy(3, CHUNKS)
                copy_result(b, 3, 0)
                tiles(b, 3, 1, TILES)

            def clear(b, i):
                if b is not None:
                    act.wait_ge(stored, 16 * (IMG * (b - 1) + i + 1) + STORED_AHEAD)
                    act.sem_inc(act_passed, 1)

            def copy_samples(b, i, t):
                if b is None:
                    return
                n = TILES * (IMG * b + i) + t
                act.wait_ge(samp_turned, n + 1 + AHEAD)
                act.wait_ge(conv3_done, n + AHEAD)
                act.copy(samp_t[:, 0:2, :], PT[:, 0:256].rearrange("p (r n) -> p r n", r=2)).then_inc(samp_sb, 1)
                act.copy(samp_t[0:C, 2, :], PT[0:C, 256:384]).then_inc(samp_sb, 1)

            def copy_result(b, i, t):
                if b is None:
                    return
                r = slice(C * i, C * (i + 1))
                act.wait_ge(conv3_done, TILES * (IMG * b + i) + t + 1 + AHEAD)
                act.copy(fin[r, bass.ds(128 * t, 128)], PO[r, 0:128]).then_inc(result_sb, 1)

            def tiles(b, i, first, end):
                for t in range(first, end):
                    copy_samples(b, i, t)
                    if t > first:
                        copy_result(b, i, t - 1)
                copy_result(b, i, end - 1)

            def image_tiles(b, i):
                clear(b, i)
                copy_samples(b, i, 0)
                with act.Fori(1, TILES) as t:
                    copy_samples(b, i, t)
                    copy_result(b, i, t - 1)
                copy_result(b, i, TILES - 1)

            schedule(act, front, image_tiles)

        @block.vector
        def _(dve):
            def norm(g, n, src, dst):
                for h in range(2):
                    dve.bn_stats(stats[:, h, :], src[:, h * 512:(h + 1) * 512])
                dve.drain()
                dve.bn_aggr(mv[:], stats[:])
                dve.drain()
                dve.tensor_scalar(ve[:], mv[:, 1:2], EPS, None, ALU.add).then_inc(var_ready, 1)
                dve.wait_ge(sd_ready, 4 * g + n + 1)
                dve.reciprocal(nr[:, 0:1], sd[:])
                dve.drain()
                dve.tensor_tensor(nr[:, 1:2], ve[:], nr[:, 0:1], ALU.mult)
                dve.drain()
                dve.tensor_scalar(nr[:, 2:3], nr[:, 1:2], sd[:], 0.5, ALU.add, ALU.mult)
                dve.drain()
                dve.reciprocal(nr[:, 3:4], nr[:, 2:3])
                dve.drain()
                return dve.tensor_scalar(dst, src if len(dst.shape) == 2 else src.rearrange("p (h w) -> p h w", w=W),
                                         mv[:, 0:1], nr[:, 3:4], ALU.subtract, ALU.mult)

            dve.sem_inc(onehot_ready, AHEAD)
            dve.memset(wg[:], 0.0)
            dve.memset(wgrid[:], 0.0)
            dve.memset(xp0[:], 0.0)
            dve.drain()
            dve.sem_inc(zeroed, 1)

            def prepare():
                for t in (xp1[:], xp3[:], bd1[:], xs2[:], cb2[C:2 * C, :], cb2[2 * C:, :]):
                    dve.memset(t, 0.0)
                dve.drain()
                dve.memset(xs2[C:C + 1, :, :], 1.0)
                dve.memset(negone[:], -1.0)
                dve.wait_ge(loaded_later, LOADS_LATER)
                dve.tensor_copy(iota[:], iota_f)
                dve.tensor_copy(ident_b[:], ident[:])
                g = grid[:].rearrange("p a (t k) -> p a t k", k=TAPS)
                bias = bgrid[:].rearrange("p (k a) -> p a k", a=2).unsqueeze(2)
                dve.tensor_tensor(g, g, bias.broadcast_to([128, 2, TILES, TAPS]), ALU.add)
                for k in range(PARTS):
                    dve.tensor_copy(codes_b[:, k, :], codes[:] if k == 0 else codes_rest)
                    dve.drain()
                    if k < PARTS - 1:
                        dve.tensor_tensor(codes_rest, codes[:] if k == 0 else codes_rest, codes_b[:, k, :],
                                          ALU.subtract)
                        dve.drain()
                dve.tensor_tensor(cbsq, cb2[0:C, :], cb2[0:C, :], ALU.mult).then_inc(sq_ready, 1)
                dve.wait_ge(norms_ready, 1)
                dve.tensor_copy(cb2[C:C + 1, :], P5[C:C + 1, :])
                dve.tensor_scalar(cb2[0:C, :], cb2[0:C, :], 2.0, None, ALU.mult)

            def front(g, b):
                tiles(b, 0, 0, 1)
                dve.wait_ge(x_loaded, 16 * (g + 1))
                grid0 = xp0[:].rearrange("p (h w) -> p h w", w=G0)
                norm(g, 0, xres[:], grid0[:, 1:H + 1, 1:W + 1])
                dve.drain()
                a = xp0[:]
                dve.tensor_reduce(rowsum[:], bass.AP(a.tensor, a.offset, [a.ap[0], [G0, G0], [PS, NV], [1, WIN]]),
                                  AX.X, ALU.add)
                dve.drain()
                a = rowsum[:]
                dve.tensor_reduce(wsum[:].rearrange("p (v h) -> p v h", h=NV),
                                  bass.AP(a.tensor, a.offset, [a.ap[0], [PS * NV, NV], [1, NV], [NV, WIN]]),
                                  AX.X, ALU.add)
                dve.drain()
                dve.tensor_scalar(wsum[:], wsum[:], 1.0 / (WIN * WIN), None, ALU.mult).then_inc(wsum_ready, 1)
                for v in range(NV):
                    a = grid0[:, PS * v:PS * v + WIN, :]
                    m = dve.tensor_copy(win[:, NV * v:NV * (v + 1), :].rearrange("p n (r q) -> p n r q", q=WIN),
                                        bass.AP(a.tensor, a.offset, [a.ap[0], [PS, NV], [G0, WIN], [1, WIN]]))
                m.then_inc(win_ready, 1)
                if b is None:
                    dve.wait_ge(loaded, LOADS)
                dve.wait_ge(feat_turned, g + 1)
                dve.tensor_copy(feat_t[:], P0[:, 128:128 + PATCHES]).then_inc(feat_sb, 1)
                dve.wait_ge(logit_ready, g + 1)
                dve.tensor_tensor(lg[:, 0], P0[0:PATCHES, 0:IMG * E0].rearrange("p (i e) -> p i e", i=IMG),
                                  bg[:], ALU.add)
                dve.drain()
                dve.tensor_reduce(mx[:, 0], lg[:, 0], AX.X, ALU.max)
                dve.drain()

                def per_image(t):
                    return t.unsqueeze(2).broadcast_to([PATCHES, IMG, E0])
                dve.tensor_tensor(lg[:, 1], lg[:, 0], per_image(mx[:, 0]), ALU.subtract).then_inc(diff_ready, 1)
                dve.tensor_tensor(lg[:, 3], lg[:, 0], per_image(mx[:, 0]), ALU.is_equal)
                dve.drain()
                dve.tensor_tensor(lg[:, 3], lg[:, 3], rank[:], ALU.mult)
                dve.drain()
                dve.tensor_reduce(mx[:, 1], lg[:, 3], AX.X, ALU.max)
                dve.drain()
                dve.tensor_tensor(lg[:, 4], lg[:, 3], per_image(mx[:, 1]), ALU.is_equal)
                dve.wait_ge(exp_ready, g + 1)
                dve.tensor_reduce(mx[:, 2], lg[:, 2], AX.X, ALU.add)
                dve.drain()
                dve.reciprocal(mx[:, 1], mx[:, 2])
                dve.drain()
                dve.tensor_tensor(lg[:, 5], lg[:, 4], per_image(mx[:, 1]), ALU.mult).then_inc(route_ready, 1)
                dve.wait_ge(route_t, g + 1)
                dve.tensor_copy(rt_t[:], P0[0:IMG * E0, 64:64 + PATCHES]).then_inc(route_t_sb, 1)
                dve.wait_ge(route_b, g + 1)
                dve.tensor_copy(rtb[:], P1[:, 0:2 * IMG * PATCHES].rearrange("p (k n) -> p k n", n=PATCHES)
                                ).then_inc(route_ready, 1)
                if b is None:
                    prepare()
                tiles(b, 0, 1, 6)
                dve.drain()

                def gate(v, i):
                    n = IMG * (NV * g + v) + i
                    dve.wait_ge(relu_done, 2 * (n + 1) + AHEAD)
                    e = ex0[:, i].rearrange("p h (n s) -> p h n s", s=PS * PS)
                    r = rtb[:, 2 * i:2 * i + 2, bass.ds(NV * v, NV)].unsqueeze(3)
                    dve.tensor_tensor(e, e, r.broadcast_to([128, 2, NV, PS * PS]), ALU.mult).then_inc(gated, 1)

                def row(v, i, t):
                    samples(b, i, t)
                    gate(v, 0)
                    gate(v, 1)
                    samples(b, i, t + 1)
                    gate(v, 2)
                    gate(v, 3)
                row(0, 0, 6)
                with dve.Fori(1, NV) as v:
                    row(v, 1, 2 * v - 2)
                tiles(b, 2, 0, 2)
                add_x(b, 0)
                add_x(b, 1)
                dve.wait_ge(y_in, 16 * 2 * IMG * (g + 1))
                for v in range(H // PS):
                    x = xres[:, PS * W * v:PS * W * (v + 1)].rearrange("p (r h q) -> p r h q", r=PS, q=PS)
                    y = yb[:, ROWN * v:ROWN * v + PS * PS * (W // PS)].rearrange("p (h r q) -> p r h q", r=PS, q=PS)
                    dve.tensor_tensor(x, x, y, ALU.add)
                dve.drain()

                grid1 = xp1[:].rearrange("p (h w) -> p h w", w=G1)[:, 1:H + 1, 1:W + 1]
                norm(g, 1, xres[:], grid1)
                dve.drain()
                dve.tensor_reduce(sm1[:, 0, 0:1], grid1, AX.XY, ALU.add)
                dve.drain()
                dve.tensor_scalar(sm1[:, 3, :], wroute[:], sm1[:, 0, 0:1], 1.0 / PIX, ALU.mult, ALU.mult
                                  ).then_inc(pooled, 1)
                dve.wait_ge(rlog_ready, g + 1)
                dve.tensor_tensor(sm1[:, 1, :], P0[:, 0:E1], broute[:], ALU.add).then_inc(z_ready, 1)
                dve.wait_ge(ez_ready, g + 1)
                dve.tensor_scalar(sm1[:, 2, :], sm1[:, 2, :], 1.0, None, ALU.add)
                dve.drain()
                dve.reciprocal(sm1[:, 0, :], sm1[:, 2, :])
                dve.drain()
                dve.tensor_scalar(mix[:], wmix[:, 0, :], sm1[:, 0, 0:1], None, ALU.mult)
                for e in range(1, E1):
                    dve.drain()
                    dve.scalar_tensor_tensor(out=mix[:], in0=wmix[:, e, :], scalar=sm1[:, 0, e:e + 1], in1=mix[:],
                                             op0=ALU.mult, op1=ALU.add)
                dve.drain()
                for i in range(IMG):
                    r = slice(C * i, C * (i + 1))
                    dve.tensor_copy(bd1[r, :, r], mix[r, :].rearrange("p (k o) -> p k o", o=C)).then_inc(bd_ready, 1)
                tiles(b, 2, 2, 5)
                for h in range(2):
                    dve.wait_ge(conv1_done, 2 * g + h + 1)
                    x = xres[:, 512 * h:512 * (h + 1)]
                    dve.tensor_tensor(x, x, PP[1 + h][:, :], ALU.add).then_inc(x2_ready, 1)
                dve.drain()
                dve.wait_ge(off_done, g)
                norm(g, 2, xres[:], xn2[:]).then_inc(xn2_ready, 1)

                def pair_of_units(t, i):
                    n = IMG * (TILES * g + t) + i
                    for j in range(2):
                        dve.wait_ge(score_done, n + j + 1 + AHEAD)
                        dve.sem_inc(dve_passed, 1)
                        dve.max(top[:, j, :], SCORES[i + j][:, :])
                    dve.drain()
                    for j in range(2):
                        dve.max_index(code[:, j, :], top[:, j, :], SCORES[i + j][:, :])
                    dve.drain()
                    for j in range(2):
                        dve.wait_ge(turned, n + j - 1 + AHEAD)
                        dve.tensor_scalar(onehot[:, j, :], iota[:], code[:, j, 0:1], None, ALU.is_equal
                                          ).then_inc(onehot_ready, 1)
                tiles(b, 2, 5, 7)
                with dve.Fori(0, TILES) as t:
                    pair_of_units(t, 0)
                    pair_of_units(t, 2)
                tiles(b, 2, 7, 8)
                for h in range(2):
                    c = slice(512 * h, 512 * (h + 1))
                    dve.wait_ge(qx_turned, 2 * g + h + 1)
                    dve.tensor_tensor(q2[:, c], PP[h][:, :], xn2[:, c], ALU.subtract)
                dve.drain()
                dve.tensor_tensor(q2[:], q2[:], xn2[:], ALU.add)
                dve.drain()
                dve.tensor_tensor(xres[:], xres[:], q2[:], ALU.add)
                dve.drain()
                dve.wait_ge(cells_t, CHUNKS * g)
                norm(g, 3, xres[:], xp3[:, 0:G1 * G1].rearrange("p (h w) -> p h w", w=G1)[:, 1:H + 1, 1:W + 1]
                     ).then_inc(xn3_ready, 1)
                if b is not None:
                    add_x(b, 2)
                    dve.tensor_copy(xlast[P - C:P, :], xfin[P - C:P, :])
                    dve.drain()
                dve.tensor_copy(xfin[:], xres[:]).then_inc(x3_ready, 1)
                if b is not None:
                    dve.tensor_copy(wlast[:], wq[:, IMG - 1])
                    dve.drain()
                samples(b, 3, 0, grant=False)
                dve.wait_ge(off_done, g + 1)

                def cells_of(i, j):
                    ht = TILES // 2
                    for h in range(2):
                        for a in range(2):
                            src = PP[h][:, 0:ht * IMG * 2 * TAPS].rearrange(
                                "p (t i k a) -> p a i t k", t=ht, i=IMG, a=2)[:, a, i:j]
                            dst = pos[:, a, i:j].rearrange("p i (t k) -> p i t k", k=TAPS)[:, :, ht * h:ht * (h + 1), :]
                            at = grid[:, a].rearrange("p (t k) -> p t k", k=TAPS)[:, ht * h:ht * (h + 1)].unsqueeze(1)
                            dve.tensor_tensor(dst, src, at.broadcast_to([128, j - i, ht, TAPS]), ALU.add)
                    dve.drain()
                    p, f, o = pos[:, :, i:j], cell[:, :, i:j], over[:, :, i:j]
                    dve.tensor_scalar(p, p, (W - 1) / 2, (W - 1) / 2 + 1, ALU.mult, ALU.add)
                    dve.drain()
                    dve.tensor_scalar(p, p, 0.0, float(W + 1), ALU.max, ALU.min)
                    dve.drain()
                    dve.tensor_scalar(f, p, float(W), WHOLE, ALU.min, ALU.add)
                    dve.drain()
                    dve.scalar_tensor_tensor(out=o, in0=f, scalar=WHOLE, in1=p, op0=ALU.subtract, op1=ALU.is_gt)
                    dve.drain()
                    dve.scalar_tensor_tensor(out=f, in0=f, scalar=WHOLE, in1=o, op0=ALU.subtract, op1=ALU.subtract)
                    dve.drain()

                def indices(i, j):
                    dve.scalar_tensor_tensor(out=idx[:, i:j].rearrange("p i t k -> p i (t k)"),
                                             in0=cell[:, 1, i:j], scalar=float(G1), in1=cell[:, 0, i:j],
                                             op0=ALU.mult, op1=ALU.add)
                cells_of(0, 1)
                indices(0, 1)
                dve.drain()
                dve.sem_inc(granted, TILES if b is None else 1)
                cells_of(1, IMG)
                indices(1, IMG if b is None else IMG - 1)
                dve.tensor_tensor(pos[:], pos[:], cell[:], ALU.subtract)
                dve.drain()
                dve.tensor_scalar(over[:], pos[:], -1.0, 1.0, ALU.mult, ALU.add)
                dve.drain()
                for q in range(CORN):
                    wy = (pos if q // 2 else over)[:, 1].rearrange("p i n -> p (i n)")
                    wx = (pos if q % 2 else over)[:, 0].rearrange("p i n -> p (i n)")
                    dve.tensor_tensor(wq[:].rearrange("p i t (k q) -> p (i t k) q", q=CORN)[:, :, q], wx, wy, ALU.mult)
                dve.drain()
                tiles(b, 3, 1, TILES)
                if b is not None:
                    indices(IMG - 1, IMG)
                    add_x(b, 3)

            def samples(b, i, t, grant=True):
                if b is None:
                    return
                n = TILES * (IMG * b + i) + t
                dve.wait_ge(tile_ready, n + 1)
                s = ring[:, bass.ds(t, 1), :].rearrange("p a (n c) -> p (a n) c", c=C)
                w = wlast[:, bass.ds(t, 1)] if i == IMG - 1 and not isinstance(b, int) else wq[:, i, bass.ds(t, 1)]
                w = w.rearrange("p a n -> p (a n)").unsqueeze(2)
                dve.tensor_tensor(s, s, w.broadcast_to([128, TAPS * CORN, C]), ALU.mult)
                dve.drain()
                s = ring[:, bass.ds(t, 1), :].rearrange("p a (k y n) -> p (a k) y n", k=TAPS, y=2)
                m = dve.tensor_tensor(pair[:].rearrange("p k x c -> p k (x c)"), s[:, :, 0], s[:, :, 1], ALU.add)
                if grant:
                    m.then_inc(granted, 1)
                dve.drain()
                dve.wait_ge(samp_turned, n + AHEAD)
                dve.tensor_tensor(samp[:].rearrange("p (k c) -> p k c", c=C), pair[:, :, 0], pair[:, :, 1],
                                  ALU.add).then_inc(samp_ready, 1)

            def add_x(b, i):
                if b is None:
                    return
                dve.wait_ge(result_sb, TILES * (IMG * b + i + 1) + AHEAD)
                src = xlast if i == IMG - 1 and not isinstance(b, int) else xfin
                r = slice(C * i, C * (i + 1))
                dve.tensor_tensor(fin[r, :], fin[r, :], src[r, :], ALU.add).then_inc(fin_ready, 1)

            def tiles(b, i, first, end):
                for t in range(first, end):
                    samples(b, i, t)

            def image_tiles(b, i):
                with dve.Fori(0, TILES) as t:
                    samples(b, i, t)
                add_x(b, i)

            schedule(dve, front, image_tiles)

        @block.tensor
        def _(pe):
            pe.sem_inc(sum0_done, AHEAD)
            pe.sem_inc(score_done, AHEAD)
            pe.sem_inc(q_done, AHEAD)
            pe.sem_inc(turned, AHEAD)
            pe.sem_inc(samp_turned, AHEAD)
            pe.sem_inc(conv3_done, AHEAD)

            def front(g, b):
                tiles(b, 0, 0, 1)
                pe.wait_ge(feat_loaded, 16 * (g + 1))
                pe.sem_inc(pe_passed, 1)
                if b is None:
                    pe.wait_ge(loaded, LOADS)
                pe.transpose(P0[:, 128:128 + PATCHES], feat[:], ident[0:PATCHES, 0:PATCHES]).then_inc(feat_turned, 1)
                pe.wait_ge(feat_sb, g + 1)
                pe.matmul(P0[0:PATCHES, 0:IMG * E0], feat_t[:], wg[:], start=True, stop=True).then_inc(logit_ready, 1)
                pe.wait_ge(route_ready, 2 * g + 1)
                pe.sem_inc(pe_passed, 1)
                pe.transpose(P0[0:IMG * E0, 64:64 + PATCHES], lg[:, 5].rearrange("p i e -> p (i e)"),
                             ident[0:PATCHES, 0:PATCHES]).then_inc(route_t, 1)
                pe.wait_ge(route_t_sb, g + 1)
                pe.wait_ge(cells_sb, CHUNKS * g)
                for k in range(2 * IMG):
                    m = pe.matmul(P1[:, PATCHES * k:PATCHES * (k + 1)], pick[:, k, :], rt_t[:], start=True, stop=True)
                m.then_inc(route_b, 1)
                if b is None:
                    pe.wait_ge(sq_ready, 1)
                    pe.matmul(P5[C:C + 1, :], negone[:], cbsq, start=True, stop=True).then_inc(norms_ready, 1)
                tiles(b, 0, 1, 6)
                pe.wait_ge(xs0_loaded, 16 * 3 * IMG * (g + 1))
                pe.sem_inc(pe_passed, 1)
                pe.wait_ge(route_ready, 2 * g + 2)
                pe.sem_inc(pe_passed, 1)

                def conv(v, i):
                    n = IMG * (NV * g + v) + i
                    pe.wait_ge(relu_done, 2 * (n - 1) + AHEAD)
                    for h in range(2):
                        for dx in range(3):
                            a = xs0[:, i, bass.ds(NV * v, NV), dx:CUT]
                            a = bass.AP(a.tensor, a.offset, [a.ap[0], [CUT, NV], [WIN, PS], [1, PS]])
                            m = pe.matmul(PP[2 * (i % 2) + h][:, 0:ROWN], w0[:, dx, h, :], a,
                                          start=(dx == 0), stop=(dx == 2))
                        m.then_inc(conv0_done, 1)

                def add_up(v):
                    pe.wait_ge(gated, IMG * (NV * g + v + 1))
                    pe.wait_ge(yc_done, NV * g + v + AHEAD)
                    for h in range(2):
                        for i in range(IMG):
                            m = pe.matmul(P4[C * i:C * (i + 1), 0:ROWN], sume[:], ex0[:, i, h, :],
                                          start=(h == 0), stop=(h == 1))
                    m.then_inc(sum0_done, 1)

                def row(v, i, t):
                    conv(v, 0)
                    if not isinstance(v, int):
                        add_up(v - 1)
                    conv(v, 1)
                    turn_samples(b, i, t)
                    conv(v, 2)
                    convolve(b, i, t)
                    turn_samples(b, i, t + 1)
                    conv(v, 3)
                    convolve(b, i, t + 1)
                row(0, 0, 6)
                with pe.Fori(1, NV) as v:
                    row(v, 1, 2 * v - 2)
                add_up(NV - 1)
                tiles(b, 2, 0, 2)

                pe.wait_ge(pooled, g + 1)
                pe.matmul(P0[:, 0:E1], same[:], sm1[:, 3, :], start=True, stop=True).then_inc(rlog_ready, 1)
                pe.wait_ge(bd_ready, IMG * (g + 1))
                grid1 = xp1[:].rearrange("p (h w) -> p h w", w=G1)
                for h in range(2):
                    for k in range(TAPS):
                        y = H // 2 * h + k // 3
                        m = pe.matmul(PP[1 + h][:, :], bd1[:, k, :], grid1[:, y:y + H // 2, k % 3:k % 3 + W],
                                      start=(k == 0), stop=(k == TAPS - 1))
                        if k == TAPS // 2:
                            turn_samples(b, 2, 2 + h)
                    m.then_inc(conv1_done, 1)
                    convolve(b, 2, 2 + h)
                tiles(b, 2, 4, 5)
                pe.wait_ge(x2_ready, 2 * (g + 1))

                def scores(t, i):
                    n = IMG * (TILES * g + t) + i
                    pe.wait_ge(staged2, n + 1)
                    pe.wait_ge(onehot_ready, n - 3 + AHEAD)
                    pe.matmul(SCORES[i][:, :], xs2[:, i, :], cb2[:], start=True, stop=True).then_inc(score_done, 1)

                def turn(t, i):
                    n = IMG * (TILES * g + t) + i
                    pe.wait_ge(onehot_ready, n + 1 + AHEAD)
                    pe.wait_ge(turned_sb, n + AHEAD)
                    for c in range(CCH):
                        m = pe.matmul(P2[:, 128 * c:128 * (c + 1)], onehot[:, i % 2, 128 * c:128 * (c + 1)],
                                      ident_b[:], start=True, stop=True)
                    m.then_inc(turned, 1)

                def pick_code(t, i):
                    n = IMG * (TILES * g + t) + i
                    pe.wait_ge(turned_sb, n + 1 + AHEAD)
                    if i == 0:
                        pe.wait_ge(qx_ready, TILES * g + t)
                    for c in range(CCH):
                        for k in range(PARTS):
                            m = pe.matmul(P4[:, C * i:C * (i + 1)], onehot_t[:, i % 2, 128 * c:128 * (c + 1)],
                                          codes_b[:, k, C * c:C * (c + 1)],
                                          start=(c == 0 and k == 0), stop=(c == CCH - 1 and k == PARTS - 1))
                    m.then_inc(q_done, 1)

                def body(t, first):
                    for i in range(IMG):
                        scores(t, i)
                        if i == 3 or not first:
                            turn(t if i == 3 else t - 1, (i - 3) % IMG)
                        if not first:
                            pick_code(t - 1, i)
                tiles(b, 2, 5, 6)
                body(0, True)
                tiles(b, 2, 6, 7)
                with pe.Fori(1, TILES) as t:
                    body(t, False)
                for t in range(TILES):
                    if t == 0:
                        pe.wait_ge(qx_ready, TILES * g + 4)
                    if t == 4:
                        for i in range(IMG):
                            if i < IMG - 1:
                                turn(TILES - 1, i + 1)
                            pick_code(TILES - 1, i)
                        pe.wait_ge(qx_ready, TILES * (g + 1))
                    m = pe.transpose(PP[t // 4][:, 128 * (t % 4):128 * (t % 4 + 1)], qx[:, t, :], ident[:])
                    if t % 4 == 3:
                        m.then_inc(qx_turned, 1)
                tiles(b, 2, 7, 8)

                def cells_of(first, end):
                    for k in range(first, end):
                        if not isinstance(g, int) or k >= 3:
                            pe.wait_ge(cells_sb, CHUNKS * g + k - 2)
                        for q in range(CORN):
                            at = 128 * k + (q // 2) * G1 + q % 2
                            m = pe.transpose(CELLS[k % 3][:, 128 * q:128 * (q + 1)], xp3[:, at:at + 128], ident[:])
                        m.then_inc(cells_t, 1)
                pe.wait_ge(flat3_ready, g + 1)
                ht = TILES // 2
                for t in range(TILES):
                    n = IMG * 2 * TAPS
                    m = pe.matmul(PP[t // ht][:, n * (t % ht):n * (t % ht + 1)],
                                  xn2[:, 128 * t:128 * (t + 1)], wgrid[:], start=True, stop=True)
                m.then_inc(off_done, 1)
                cells_of(0, 3)
                turn_samples(b, 3, 0)
                cells_of(3, CHUNKS)
                convolve(b, 3, 0)
                tiles(b, 3, 1, TILES)

            def convolve(b, i, t):
                if b is None:
                    return
                n = TILES * (IMG * b + i) + t
                pe.wait_ge(samp_sb, 2 * (n + 1))
                pe.wait_ge(result_sb, n + AHEAD)
                for r in range(3):
                    k = min(128, TC - 128 * r)
                    m = pe.matmul(PO[C * i:C * (i + 1), 0:128], wc[0:k, r, :], samp_t[0:k, r, :],
                                  start=(r == 0), stop=(r == 2))
                m.then_inc(conv3_done, 1)

            def turn_samples(b, i, t):
                if b is None:
                    return
                pe.wait_ge(samp_ready, TILES * (IMG * b + i) + t + 1)
                for r in range(3):
                    k = min(128, TC - 128 * r)
                    m = pe.transpose(PT[0:k, 128 * r:128 * (r + 1)], samp[:, 128 * r:128 * r + k], ident[:])
                m.then_inc(samp_turned, 1)

            def tiles(b, i, first, end):
                for t in range(first, end):
                    if t > first:
                        convolve(b, i, t - 1)
                    turn_samples(b, i, t)
                convolve(b, i, end - 1)

            def image_tiles(b, i):
                turn_samples(b, i, 0)
                with pe.Fori(1, TILES) as t:
                    convolve(b, i, t - 1)
                    turn_samples(b, i, t)
                convolve(b, i, TILES - 1)

            schedule(pe, front, image_tiles)


LOADS = 16 * (9 + 2 * IMG)
LOADS_LATER = 16 * (2 * IMG + 5 + 3)


def constants():
    f = np.float32
    pick = np.zeros((IMG * E0, 2 * IMG, 128), f)
    for i in range(IMG):
        for e in range(E0):
            pick[i * E0 + e, 2 * i + e // HALF, (e % HALF) * C:(e % HALF + 1) * C] = 1
    grid = np.zeros((128, 2, TILES, TAPS), f)
    base = np.linspace(-1.0, 1.0, W, dtype=f)
    koff = np.linspace(-2 / (W - 1), 2 / (W - 1), 3, dtype=f)
    for t in range(TILES):
        for p in range(128):
            y, x = divmod(128 * t + p, W)
            for k in range(TAPS):
                grid[p, 0, t, k] = base[x] + koff[k % 3]
                grid[p, 1, t, k] = base[y] + koff[k // 3]
    return {
        "ident": np.eye(128, dtype=f),
        "pick_expert": pick,
        "sum_experts": np.tile(np.eye(C, dtype=f), (HALF, 1)),
        "same_image": np.kron(np.eye(IMG, dtype=f), np.ones((C, C), f)),
        "code_iota": np.tile(np.arange(CODES, dtype=f), (128, 1)),
        "first_rank": np.tile(np.arange(E0, 0, -1, dtype=f), (PATCHES, IMG, 1)),
        "grid": grid.reshape(128, 2, TILES * TAPS),
    }


def kernel(**inputs):
    import concourse.bacc as bacc
    from concourse.bass_utils import run_bass_kernel_spmd

    a = {k: np.asarray(v) for k, v in inputs.items()}
    arrays = {
        "x": a["x"].reshape(B * C, PIX),
        "Wg": a["L0_conv_Wg"],
        "bg": np.broadcast_to(a["L0_conv_bg"], (IMG, E0)),
        "Wexp": a["L0_conv_Wexp"].transpose(3, 2, 4, 0, 1).reshape(3 * C, 3, 2, HALF * C),
        "bexp": a["L0_conv_bexp"].reshape(2, HALF * C).T,
        "w_route": a["L1_conv_w_route"].T,
        "b_route": a["L1_conv_b_route"],
        "w_mix": a["L1_conv_w_experts"].transpose(2, 0, 3, 4, 1).reshape(C, E1, TC),
        "codebook": a["L2_conv_codebook"],
        "codebook_t": a["L2_conv_codebook"].T,
        "w_grid": a["L3_conv_w_grid"].T,
        "b_grid": a["L3_conv_b_grid"],
        "w_conv": a["L3_conv_w_conv"].transpose(2, 3, 1, 0).reshape(TC, C),
    }
    arrays.update(constants())
    arrays = {f"in_{k}": np.ascontiguousarray(v) for k, v in arrays.items()}
    nc = bacc.Bacc("TRN2", target_bir_lowering=False, num_devices=1)
    aps = {k: nc.dram_tensor(f"in_{k}", arrays[f"in_{k}"].shape, mybir.dt.from_np(arrays[f"in_{k}"].dtype),
                             kind="ExternalInput").ap() for k in INPUTS}
    aps["out"] = nc.dram_tensor("out", (B * C, PIX), F32, kind="ExternalOutput").ap()
    build(nc, aps)
    r = run_bass_kernel_spmd(nc, [arrays], core_ids=[0])
    return r.results[0]["out"].reshape(B, C, H, W)
```
